# Optimizing a Trainium2 kernel written in Bass

```python
import numpy as np
import jax
import jax.numpy as jnp

def _softmax(x, axis=-1):
    return jax.nn.softmax(x, axis=axis)

def _gelu(x):
    return jax.nn.gelu(x, approximate=True)

def _silu(x):
    return jax.nn.silu(x)

def _sigmoid(x):
    return jax.nn.sigmoid(x)

def _layernorm(x, axis=-1, eps=1e-05):
    m = jnp.mean(x, axis=axis, keepdims=True)
    v = jnp.var(x, axis=axis, keepdims=True)
    return (x - m) / jnp.sqrt(v + eps)

def _scatter_add(tgt, idx, src, axis=0):
    return tgt.at[idx].add(src)

def _segment_sum(src, seg, n):
    return jax.ops.segment_sum(src, seg, n)
kernel_name = 'mk_gnn_preln_d2_gnn_r8_20d13c'

def setup_inputs(seed: int=0):
    np.random.seed(seed)
    _w = jnp.asarray

    def _rec_inputs():
        import jax
        import jax.numpy as jnp
        _gk = jax.random.key(seed)
        x = -6.985e-05 + 0.9998 * jax.random.normal(jax.random.fold_in(_gk, 1), (1250, 512), jnp.float32)
        src = jax.random.randint(jax.random.fold_in(_gk, 2), (20000,), 0, 1250, jnp.int32)
        dst = jax.random.randint(jax.random.fold_in(_gk, 3), (20000,), 0, 1250, jnp.int32)
        _o = jnp.argsort(dst, stable=True)
        src = src[_o]
        dst = dst[_o]
        return (x, src, dst)
    x, src, dst = _rec_inputs()

    def _L0_gnn_setup():
        import jax, jax.numpy as jnp
        import numpy as np
        B = 32
        MAXN = 256
        HEADS = 8
        DH = 64
        M = 256
        D = 512
        EPS = 1e-05
        KEPS = 1e-06

        def _batchnorm(x, g, b):
            mu = jnp.mean(x, axis=0)
            var = jnp.mean((x - mu) ** 2, axis=0)
            return (x - mu) * jax.lax.rsqrt(var + EPS) * g + b

        def _forward(x, batch, edge_index, norm1_g, norm1_b, norm2_g, norm2_b, W_conv, b_conv, Wq, Wk, Wv, Wo, proj):
            N = x.shape[0]
            E = edge_index.shape[1]
            h = x
            xn = _batchnorm(x, norm1_g, norm1_b)
            msg = xn[edge_index[0]]
            agg = jax.ops.segment_sum(msg, edge_index[1], num_segments=N)
            deg = jax.ops.segment_sum(jnp.ones((E,), x.dtype), edge_index[1], num_segments=N)
            agg = agg / jnp.maximum(deg, 1.0)[:, None]
            conv_out = jax.nn.relu(agg @ W_conv + b_conv)
            counts = jax.ops.segment_sum(jnp.ones((N,), jnp.int32), batch, num_segments=B)
            offsets = jnp.concatenate([jnp.zeros((1,), jnp.int32), jnp.cumsum(counts)[:-1]])
            pos = jnp.arange(N, dtype=jnp.int32) - offsets[batch]
            h_dense = jnp.zeros((B, MAXN, D), x.dtype).at[batch, pos].set(h)
            mask = jnp.zeros((B, MAXN), bool).at[batch, pos].set(True)

            def heads(t, W):
                return (t @ W).reshape(B, MAXN, HEADS, DH).transpose(0, 2, 1, 3)
            q, k, v = (heads(h_dense, Wq), heads(h_dense, Wk), heads(h_dense, Wv))
            scale = DH ** (-0.25)

            def phi(t, is_query):
                t = t * scale
                u = jnp.einsum('bhnd,md->bhnm', t, proj)
                diag = 0.5 * jnp.sum(t * t, axis=-1, keepdims=True)
                if is_query:
                    m_ = jnp.max(u, axis=-1, keepdims=True)
                else:
                    m_ = jnp.max(u, axis=(-2, -1), keepdims=True)
                return jnp.exp(u - diag - jax.lax.stop_gradient(m_)) / np.sqrt(M) + KEPS
            qf = phi(q, True)
            kf = phi(k, False) * mask[:, None, :, None]
            vm = v * mask[:, None, :, None]
            kv = jnp.einsum('bhnm,bhnd->bhmd', kf, vm)
            z = 1.0 / (jnp.einsum('bhnm,bhm->bhn', qf, kf.sum(axis=2)) + KEPS)
            attn = jnp.einsum('bhnm,bhmd->bhnd', qf, kv) * z[..., None]
            attn = attn.transpose(0, 2, 1, 3).reshape(B, MAXN, D) @ Wo
            h_attn = attn[batch, pos]
            return _batchnorm(conv_out + h_attn + h, norm2_g, norm2_b)
        key = jax.random.key(seed)
        ks = jax.random.split(key, 10)
        sizes = 1024 + np.arange(B) * 131 % 1025
        N = int(sizes.sum())
        E = N * 8
        batch = jnp.asarray(np.repeat(np.arange(B), sizes), dtype=jnp.int32)
        edge_index = jax.random.randint(ks[0], (2, E), 0, N, dtype=jnp.int32)
        s = 1.0 / np.sqrt(D)
        return {'x': jax.random.normal(ks[1], (N, D), jnp.float32), 'batch': batch, 'edge_index': edge_index, 'norm1_g': jnp.ones((D,), jnp.float32), 'norm1_b': jnp.zeros((D,), jnp.float32), 'norm2_g': jnp.ones((D,), jnp.float32), 'norm2_b': jnp.zeros((D,), jnp.float32), 'W_conv': jax.random.normal(ks[2], (D, D), jnp.float32) * s, 'b_conv': jnp.zeros((D,), jnp.float32), 'Wq': jax.random.normal(ks[3], (D, D), jnp.float32) * s, 'Wk': jax.random.normal(ks[4], (D, D), jnp.float32) * s, 'Wv': jax.random.normal(ks[5], (D, D), jnp.float32) * s, 'Wo': jax.random.normal(ks[6], (D, D), jnp.float32) * s, 'proj': jax.random.normal(ks[7], (M, DH), jnp.float32)}
    _L0_gnn_all = _L0_gnn_setup()
    _L0_gnn_in = {k: v for k, v in _L0_gnn_all.items() if k in ('norm1_g', 'norm1_b', 'norm2_g', 'norm2_b', 'W_conv', 'b_conv', 'Wq', 'Wk', 'Wv', 'Wo', 'proj')}
    del _L0_gnn_all

    def _L1_gnn_setup():
        import jax, jax.numpy as jnp
        import numpy as np
        BN_EPS = 1e-05

        def batch_norm(h, gamma, beta):
            mu = jnp.mean(h, axis=0)
            var = jnp.var(h, axis=0)
            return (h - mu) * jax.lax.rsqrt(var + BN_EPS) * gamma + beta
        key = jax.random.key(seed)
        ks = jax.random.split(key, 6)
        N, E, dim = (6250, 200000, 512)
        hidden = dim * 2
        x = jax.random.normal(ks[0], (N, dim), dtype=jnp.float32)
        edge_index = jax.random.randint(ks[1], (2, E), 0, N, dtype=jnp.int64)
        s1 = 1.0 / np.sqrt(dim)
        s2 = 1.0 / np.sqrt(hidden)
        return {'x': x, 'edge_index': edge_index, 'eps': jnp.float32(0.0), 'W1': jax.random.uniform(ks[2], (dim, hidden), jnp.float32, -s1, s1), 'b1': jnp.zeros((hidden,), jnp.float32), 'g1': jnp.ones((hidden,), jnp.float32), 'be1': jnp.zeros((hidden,), jnp.float32), 'W2': jax.random.uniform(ks[3], (hidden, dim), jnp.float32, -s2, s2), 'b2': jnp.zeros((dim,), jnp.float32), 'g2': jnp.ones((dim,), jnp.float32), 'be2': jnp.zeros((dim,), jnp.float32)}
    _L1_gnn_all = _L1_gnn_setup()
    _L1_gnn_in = {k: v for k, v in _L1_gnn_all.items() if k in ('eps', 'W1', 'b1', 'g1', 'be1', 'W2', 'b2', 'g2', 'be2')}
    del _L1_gnn_all
    return {'x': x, 'src': src, 'dst': dst, 'L0_gnn_norm1_g': _L0_gnn_in['norm1_g'], 'L0_gnn_norm1_b': _L0_gnn_in['norm1_b'], 'L0_gnn_norm2_g': _L0_gnn_in['norm2_g'], 'L0_gnn_norm2_b': _L0_gnn_in['norm2_b'], 'L0_gnn_W_conv': _L0_gnn_in['W_conv'], 'L0_gnn_b_conv': _L0_gnn_in['b_conv'], 'L0_gnn_Wq': _L0_gnn_in['Wq'], 'L0_gnn_Wk': _L0_gnn_in['Wk'], 'L0_gnn_Wv': _L0_gnn_in['Wv'], 'L0_gnn_Wo': _L0_gnn_in['Wo'], 'L0_gnn_proj': _L0_gnn_in['proj'], 'L1_gnn_eps': _L1_gnn_in['eps'], 'L1_gnn_W1': _L1_gnn_in['W1'], 'L1_gnn_b1': _L1_gnn_in['b1'], 'L1_gnn_g1': _L1_gnn_in['g1'], 'L1_gnn_be1': _L1_gnn_in['be1'], 'L1_gnn_W2': _L1_gnn_in['W2'], 'L1_gnn_b2': _L1_gnn_in['b2'], 'L1_gnn_g2': _L1_gnn_in['g2'], 'L1_gnn_be2': _L1_gnn_in['be2']}

def reference(x, src, dst, L0_gnn_norm1_g, L0_gnn_norm1_b, L0_gnn_norm2_g, L0_gnn_norm2_b, L0_gnn_W_conv, L0_gnn_b_conv, L0_gnn_Wq, L0_gnn_Wk, L0_gnn_Wv, L0_gnn_Wo, L0_gnn_proj, L1_gnn_eps, L1_gnn_W1, L1_gnn_b1, L1_gnn_g1, L1_gnn_be1, L1_gnn_W2, L1_gnn_b2, L1_gnn_g2, L1_gnn_be2):
    import jax
    import jax.numpy as jnp

    def _L0_gnn_ref(x, batch, edge_index, norm1_g, norm1_b, norm2_g, norm2_b, W_conv, b_conv, Wq, Wk, Wv, Wo, proj):
        import jax, jax.numpy as jnp
        import numpy as np
        B = 32
        MAXN = 256
        HEADS = 8
        DH = 64
        M = 256
        D = 512
        EPS = 1e-05
        KEPS = 1e-06

        def _batchnorm(x, g, b):
            mu = jnp.mean(x, axis=0)
            var = jnp.mean((x - mu) ** 2, axis=0)
            return (x - mu) * jax.lax.rsqrt(var + EPS) * g + b

        def _forward(x, batch, edge_index, norm1_g, norm1_b, norm2_g, norm2_b, W_conv, b_conv, Wq, Wk, Wv, Wo, proj):
            N = x.shape[0]
            E = edge_index.shape[1]
            h = x
            xn = _batchnorm(x, norm1_g, norm1_b)
            msg = xn[edge_index[0]]
            agg = jax.ops.segment_sum(msg, edge_index[1], num_segments=N)
            deg = jax.ops.segment_sum(jnp.ones((E,), x.dtype), edge_index[1], num_segments=N)
            agg = agg / jnp.maximum(deg, 1.0)[:, None]
            conv_out = jax.nn.relu(agg @ W_conv + b_conv)
            counts = jax.ops.segment_sum(jnp.ones((N,), jnp.int32), batch, num_segments=B)
            offsets = jnp.concatenate([jnp.zeros((1,), jnp.int32), jnp.cumsum(counts)[:-1]])
            pos = jnp.arange(N, dtype=jnp.int32) - offsets[batch]
            h_dense = jnp.zeros((B, MAXN, D), x.dtype).at[batch, pos].set(h)
            mask = jnp.zeros((B, MAXN), bool).at[batch, pos].set(True)

            def heads(t, W):
                return (t @ W).reshape(B, MAXN, HEADS, DH).transpose(0, 2, 1, 3)
            q, k, v = (heads(h_dense, Wq), heads(h_dense, Wk), heads(h_dense, Wv))
            scale = DH ** (-0.25)

            def phi(t, is_query):
                t = t * scale
                u = jnp.einsum('bhnd,md->bhnm', t, proj)
                diag = 0.5 * jnp.sum(t * t, axis=-1, keepdims=True)
                if is_query:
                    m_ = jnp.max(u, axis=-1, keepdims=True)
                else:
                    m_ = jnp.max(u, axis=(-2, -1), keepdims=True)
                return jnp.exp(u - diag - jax.lax.stop_gradient(m_)) / np.sqrt(M) + KEPS
            qf = phi(q, True)
            kf = phi(k, False) * mask[:, None, :, None]
            vm = v * mask[:, None, :, None]
            kv = jnp.einsum('bhnm,bhnd->bhmd', kf, vm)
            z = 1.0 / (jnp.einsum('bhnm,bhm->bhn', qf, kf.sum(axis=2)) + KEPS)
            attn = jnp.einsum('bhnm,bhmd->bhnd', qf, kv) * z[..., None]
            attn = attn.transpose(0, 2, 1, 3).reshape(B, MAXN, D) @ Wo
            h_attn = attn[batch, pos]
            return _batchnorm(conv_out + h_attn + h, norm2_g, norm2_b)
        return _forward(x, batch, edge_index, norm1_g, norm1_b, norm2_g, norm2_b, W_conv, b_conv, Wq, Wk, Wv, Wo, proj)

    def _L1_gnn_ref(x, edge_index, eps, W1, b1, g1, be1, W2, b2, g2, be2):
        import jax, jax.numpy as jnp
        import numpy as np
        BN_EPS = 1e-05

        def batch_norm(h, gamma, beta):
            mu = jnp.mean(h, axis=0)
            var = jnp.var(h, axis=0)
            return (h - mu) * jax.lax.rsqrt(var + BN_EPS) * gamma + beta
        N = x.shape[0]
        src, dst = (edge_index[0], edge_index[1])
        agg = jax.ops.segment_sum(x[src], dst, num_segments=N)
        h = (1.0 + eps) * x + agg
        h = jax.nn.relu(batch_norm(h @ W1 + b1, g1, be1))
        h = h @ W2 + b2
        h = jax.nn.relu(batch_norm(h, g2, be2))
        return x + h
    edge_index = jnp.stack([src, dst])
    batch0 = jnp.zeros((1250,), jnp.int32)
    h = jnp.maximum(_layernorm(x, axis=-1), 0.0)
    x = x + _L0_gnn_ref(h, batch0, edge_index, L0_gnn_norm1_g, L0_gnn_norm1_b, L0_gnn_norm2_g, L0_gnn_norm2_b, L0_gnn_W_conv, L0_gnn_b_conv, L0_gnn_Wq, L0_gnn_Wk, L0_gnn_Wv, L0_gnn_Wo, L0_gnn_proj)
    h = jnp.maximum(_layernorm(x, axis=-1), 0.0)
    x = x + _L1_gnn_ref(h, edge_index, L1_gnn_eps, L1_gnn_W1, L1_gnn_b1, L1_gnn_g1, L1_gnn_be1, L1_gnn_W2, L1_gnn_b2, L1_gnn_g2, L1_gnn_be2)
    return x

_drawn_inputs = setup_inputs


def setup_inputs(seed=0):
    import zlib

    import numpy as np

    out = dict(_drawn_inputs(seed))
    spreads = {'L0_gnn_norm1_g': (1.0, 0.2),
     'L0_gnn_norm1_b': (0.0, 0.1),
     'L0_gnn_norm2_g': (1.0, 0.2),
     'L0_gnn_norm2_b': (0.0, 0.1),
     'L0_gnn_b_conv': (0.0, 0.1),
     'L1_gnn_b1': (0.0, 2.0),
     'L1_gnn_g1': (1.0, 0.2),
     'L1_gnn_be1': (0.0, 0.394),
     'L1_gnn_b2': (0.0, 2.0),
     'L1_gnn_g2': (1.0, 0.2),
     'L1_gnn_be2': (0.0, 0.307)}
    factors = {'L0_gnn_Wq': 29.768,
     'L0_gnn_Wk': 3.614,
     'L0_gnn_Wv': 29.464,
     'L0_gnn_Wo': 29.856,
     'L0_gnn_proj': 32.568}
    for name, (base, spread) in spreads.items():
        noise = np.random.default_rng([zlib.crc32(name.encode()), seed]).standard_normal(out[name].shape)
        drawn = base * np.exp(spread * noise) if base else spread * noise
        out[name] = jnp.asarray(drawn.astype(out[name].dtype))
    for name, factor in factors.items():
        out[name] = (out[name] * factor).astype(out[name].dtype)
    return out
```

```python
from contextlib import ExitStack

import concourse.bass as bass
from concourse import mybir

F32 = mybir.dt.float32
F32R = mybir.dt.float32r
F16 = mybir.dt.float16
F8 = mybir.dt.float8e4
I32 = mybir.dt.int32
U8 = mybir.dt.uint8
ALU = mybir.AluOpType
ACT = mybir.ActivationFunctionType
AX = mybir.AxisListType

P = 128
KIB = 1024

N, D, HID, E = 1250, 512, 1024, 20000
HEADS, DH, M, MAXN = 8, 64, 256, 256
LN_EPS = BN_EPS = 1e-5
KEPS = 1e-6

T = 10
L = N // T
FB = D // P
HB = HID // P
CH = 125
NCH = E // CH
G = 8
Q = 4
W = 50
NW = N // W
CODES = T * W
BIG = 16
COLS = [(0, 418), (418, 416), (834, 416)]
NC = len(COLS)
PIECE = 2 * L
WIN_SHIFT, WIN_MUL = 16, 1311
TILE_SHIFT, TILE_MUL = 17, 1049
assert all(d * WIN_MUL >> WIN_SHIFT == d // W and d * TILE_MUL >> TILE_SHIFT == d // L for d in range(N))
assert NCH == 160 and L * T == N and W * NW == N and CODES <= 512 and BIG * CH <= 2048

PARAMS = [("n1g", FB), ("n1b", FB), ("n2g", FB), ("n2b", FB), ("bc", FB),
          ("b1", HB), ("g1", HB), ("be1", HB), ("b2", FB), ("g2", FB), ("be2", FB)]
NPAR = sum(n for _, n in PARAMS)
PAR0 = {}
for _n, _k in PARAMS:
    PAR0[_n] = sum(k for _, k in PARAMS[:len(PAR0)])

SLOTS = [s.split() for s in (
    "PT V0", "V1 Q0", "Q1 K0", "K1", "DG UK0", "UK1 UK2", "UK3 UQ0", "UQ1", "KV0 KV1", "QT0 QT1", "UK4 UK5",
    "UK6 UK7", "O0 UQ2", "UQ3 KV2", "KV3 QT2", "QT3 UQ4", "UQ5 O1", "QT4", "QT5 UQ6", "UQ7 O2", "QT6 QT7",
    "O3", "AT0 AT1", "WO0 WO1", "")]
ATT = [name for slot in SLOTS for name in slot]
assert len(SLOTS) == NW


def conv_order():
    out = [("A", f, 0) for f in range(FB)]
    for c in range(NC):
        if c + 1 < NC:
            out += [("A", f, c + 1) for f in range(FB)]
        out += [("C", f, c) for f in range(FB)]
    return out


CONV = conv_order()
A1_FIRST = [(f, c) for f in (0, 1) for c in range(NC)]
A1_REST = [(f, c) for c in range(NC) for f in (2, 3)]


def plan_banks():
    place, used = {}, [0] * 8

    def take(name, bank):
        place[name] = (bank, used[bank])
        used[bank] += 1

    take("codes", 2)
    take("ranges", 3)
    take("rowranges", 4)
    for i in range(T):
        take(f"hT{i}", 4 + i % 4)
    for n, name in enumerate(ATT):
        take(name, 2 + n % 6)
    take("deg", 6)
    for j in range(6):
        take(f"degb{j}", j)
    for n, (kind, f, c) in enumerate(CONV):
        take(f"{kind}{f}{c}", n % 8)
    for n, (f, c) in enumerate(A1_FIRST):
        take(f"B{f}{c}", n)
    for i in range(T):
        take(f"x{i}", 6)
        take(f"g{i}", 7)
    for n, (f, c) in enumerate(A1_REST):
        take(f"B{f}{c}", n)
    n = 6
    for b in range(HB):
        for c in range(NC):
            take(f"Z{b}{c}", n % 8)
            n += 1
    n = 0
    for f in range(FB):
        for c in range(NC):
            take(f"U{f}{c}", n % 6)
            n += 1
        for j in range(3):
            take(f"out{f}{j}", 6 + (3 * f + j) % 2)
    return place


PLACE = plan_banks()
OUT_TILES = [(0, 4), (4, 8), (8, 10)]


class Own:

    def __init__(self, eng, sem):
        self.eng, self.sem, self.n = eng, sem, 0

    def mark(self, ins):
        self.n += 1
        ins.then_inc(self.sem, 1)
        return self.n

    def after(self, n):
        self.eng.wait_ge(self.sem, n)

    def step(self, ins):
        self.after(self.mark(ins))


def gnn_kernel(nc, x, src, dst, params, eps, w_conv, wq, wk, wv, wo, proj, w1, w2, out):
    with ExitStack() as ctx:
        sems = {}

        def sem(name):
            if name not in sems:
                sems[name] = ctx.enter_context(nc.semaphore(name))
            return sems[name]

        def place(name, shape, dt, kib):
            pad = nc.sbuf_tensor(name + "_at", [P, int(kib * KIB)], U8)
            pad.__enter__()
            it = nc.sbuf_tensor(name, shape, dt)
            t = it.__enter__()
            it.__exit__(None, None, None)
            pad.__exit__(None, None, None)
            return t

        iota_code = place("iota_code", [P, CODES], F16, 0.25)
        iota_lane = place("iota_lane", [P, P, G], F16, 1.25)
        ones16 = place("ones16", [P, P], F16, 3.25)
        zeros16 = place("zeros16", [P, CODES], F16, 3.5)
        ident = place("ident", [P, P], F32, 4.5)
        chunk_down = place("chunk_down", [NW, NCH], F32, 5)
        chunk_up = place("chunk_up", [NW, NCH], F32, 5.625)
        par = place("par", [P, NPAR], F32, 6.25)
        half2 = place("half2", [P, 2], F32, 6.5)
        minus_half = place("minus_half", [P, T], F32, 6.53125)
        win_of_lane = place("win_of_lane", [NW, 1], F32, 6.59375)
        eps1 = place("eps1", [P, 1], F32, 6.625)
        eps_col = place("eps_col", [P, 1], F32, 6.65625)
        ranges = place("ranges", [1, NW, 2], I32, 6.6875)
        most = place("most", [1, 1], I32, 6.90625)
        neg_bc = place("neg_bc", [P, FB], F32, 6.9375)
        rng_f = place("rng_f", [1, 4, NW], F32, 7)
        red = place("red", [NW, 2], F32, 7.40625)
        wm = place("wm", [P, 2, 2], F32, 7.4375)
        st_row = place("st_row", [L, 2, 6], F32, 7.46875)
        att255 = place("att255", [P, FB], F32, 7.5625)
        st_f = place("st_f", [P, HB, NC, 6], F32, 86.25)
        mv_f = place("mv_f", [P, HB, 2], F32, 86.84375)
        mv_row = place("mv_row", [L, T, 2], F32, 86.90625)
        bn_tmp = place("bn_tmp", [P, 2, HB], F32, 87)
        bn_s = place("bn_s", [P, HB], F32, 87.09375)
        bn_t = place("bn_t", [P, HB], F32, 87.125)
        ln_tmp = place("ln_tmp", [L, 2, T], F32, 87.15625)
        ln_s = place("ln_s", [L, T], F32, 87.25)
        ln_b = place("ln_b", [L, T], F32, 87.3125)
        kmax = place("kmax", [P, HEADS, 2], F32, 87.375)
        kmax1 = place("kmax1", [P, HEADS], F32, 87.4375)
        kmaxall = place("kmaxall", [P, HEADS], F32, 87.46875)
        nbk = place("nbk", [P, HEADS, 2], F32, 87.5)
        nbq = place("nbq", [P, HEADS, 2], F32, 87.5625)
        qmax = place("qmax", [P, HEADS, 2], F32, 87.625)
        zden = place("zden", [P, 2, 4], F32, 87.6875)
        diag = place("diag", [P, 2, HEADS, 2], F32, 87.75)
        deg2 = place("deg2", [L, 3, T], F32, 87.875)
        AT = place("AT", [L, T, N], F16, 8)
        ATlo = place("ATlo", [L, T, N], F8, 32.5)
        ATlo_words = place("ATlo_words", [L, T * N // 4], I32, 32.5)
        hh = place("hh", [L, T, D], F16, 45)
        hl = place("hl", [L, T, D], F16, 55)
        hT = place("hT", [P, FB, N], F32, 65)
        S = place("S", [CH, P, NCH + G], F16, 88)
        ring = place("ring", [CH, G, CODES], F16, 130)
        tqk = place("tqk", [P, 2, FB, MAXN], F32, 138)
        sq = place("sq", [P, 2, FB, MAXN], F32, 146)
        wA = place("wA", [P, FB, D], F32, 154)
        wB = place("wB", [P, FB, D], F32, 162)
        vaug = place("vaug", [P, 2, HEADS, DH + 1], F32, 170)
        attn = place("attn", [P, 2, D], F32, 174.25)
        attnT = place("attnT", [P, FB, MAXN], F32, 178.25)
        hring = place("hring", [L, 3, D], F32, 182.25)
        xring = place("xring", [L, 4, D], F32, 188.25)
        edge = place("edge", [P, 2, 2, CH], I32, 196.25)
        quo = place("quo", [P, 2, 2, CH], I32, 198.25)
        code_r = place("code_r", [P, 3, 2, CH], F32, 200.25)
        kf = place("kf", [P, 4, 2, M], F32, 182.25)
        qf = place("qf", [P, 2, 2, M], F32, 190.25)
        qfT = place("qfT", [P, 2, 2, MAXN], F32, 194.25)
        kv = place("kv", [P, HEADS, 2, DH + 1], F32, 198.25)
        projT = place("projT", [P, M], F32, 203.25)
        proj_d = place("proj_d", [P, 2, P], F32, 204.25)
        par_r = place("par_r", [NPAR, P], F32, 205.25)
        code = place("code", [CH, NCH + G], F32, 205.75)
        slo = place("slo", [CH, NCH + G], F16, 206.4375)
        sel = place("sel", [NW, 2, NCH], F32, 85)
        agg_hi = place("agg_hi", [P, FB, N], F32R, 88)
        agg_lo = place("agg_lo", [P, FB, N], F32R, 107.5625)
        tmpr = place("tmpr", [P, 2, COLS[0][1]], F32, 127.25)
        aggf = place("aggf", [P, 4, COLS[0][1]], F32, 130.75)
        rdb = place("rdb", [P, N], F32, 138)
        indb = place("indb", [P, N], F32, 143)
        wc_hi = place("wc_hi", [P, FB, D], F32R, 182.25)
        wc_lo = place("wc_lo", [P, FB, D], F32R, 190.25)
        x1 = place("x1", [L, T, D], F32, 154)
        w1_hi = place("w1_hi", [P, FB, HID], F32R, 138)
        w1_lo = place("w1_lo", [P, FB, HID], F32R, 174)
        w1_s = place("w1_s", [P, 2, HID], F32, 190)
        hring1 = place("hring1", [L, 3, D], F32, 198.25)
        a_hi = place("a_hi", [P, HB, N], F32R, 8)
        a_lo = place("a_lo", [P, HB, N], F32R, 47.125)
        zr = place("zr", [P, 2, N], F32, 127.25)
        w20_s = place("w20_s", [P, HB, P], F32, 190)
        w20_hi = place("w20_hi", [P, HB, P], F32R, 194)
        w20_lo = place("w20_lo", [P, HB, P], F32R, 198)
        w2_s = place("w2_s", [P, HB, 3 * P], F32, 88)
        w2_hi = place("w2_hi", [P, HB, 3 * P], F32R, 100)
        w2_lo = place("w2_lo", [P, HB, 3 * P], F32R, 112)
        ur = place("ur", [P, 2, N], F32, 138)
        orr = place("orr", [P, 2, N], F32, 174)

        banks = [ctx.enter_context(nc.psum_tensor(f"bank{i}", [P, 512], F32)) for i in range(8)]

        full = [sem(f"full{i}") for i in range(8)]
        free = [sem(f"free{i}") for i in range(8)]

        def open_group(eng, name):
            bank, turn = PLACE[name]
            if turn:
                eng.wait_ge(free[bank], turn)
            return banks[bank]

        def close_group(ins, name):
            ins.then_inc(full[PLACE[name][0]], 1)

        def read_group(eng, name):
            bank, turn = PLACE[name]
            eng.wait_ge(full[bank], turn + 1)
            return banks[bank]

        def free_group(ins, name):
            ins.then_inc(free[PLACE[name][0]], 1)

        def pcol(name, k=0, n=1):
            return par[:, PAR0[name] + k:PAR0[name] + k + n]

        x_t = x.rearrange("(t l) d -> t l d", l=L)
        out_t = out.rearrange("(t l) d -> l t d", l=L)
        dst_t, src_t = (a.rearrange("(c e) -> c e", e=CH) for a in (dst, src))

        def w_t(w):
            return w.rearrange("(k p) n -> p k n", p=P)

        NCONST = 14
        block = ctx.enter_context(nc.Block())

        @block.sync
        def _(sp):
            for a, d in enumerate((dst_t, src_t)):
                sp.dma_start(edge[:, a, 0, :], d[0:P, :]).then_inc(sem("d_edge"), 16)
            sp.wait_ge(sem("s_epad"), 1)
            for a, d in enumerate((dst_t, src_t)):
                sp.dma_start(edge[0:NCH - P, a, 1, :], d[P:NCH, :]).then_inc(sem("d_edge"), 16)
            for i in range(4):
                sp.dma_start(xring[:, i % 4, :], x_t[i]).then_inc(sem(f"d_x{i % 4}"), 16)
            sp.dma_start(wA[:], w_t(wv)).then_inc(sem("d_wA"), 16)
            sp.dma_start(wB[:], w_t(wq)).then_inc(sem("d_wB"), 16)
            for i in range(4, T):
                sp.wait_ge(sem("s_hh"), i - 3)
                sp.dma_start(xring[:, i % 4, :], x_t[i]).then_inc(sem(f"d_x{i % 4}"), 16)
            sp.wait_ge(full[PLACE["V1"][0]], PLACE["V1"][1] + 1)
            sp.dma_start(wA[:], w_t(wk)).then_inc(sem("d_wA"), 16)
            sp.wait_ge(full[PLACE["Q1"][0]], PLACE["Q1"][1] + 1)
            sp.dma_start(wB[:], w_t(wo)).then_inc(sem("d_wB"), 16)
            sp.wait_ge(full[PLACE["K1"][0]], PLACE["K1"][1] + 1)
            sp.dma_start(wA[:], w_t(w_conv)).then_inc(sem("d_wA"), 16)
            sp.wait_ge(full[PLACE["WO1"][0]], PLACE["WO1"][1] + 1)
            sp.wait_ge(sem("s_wc"), 1)
            for half in range(2):
                sp.dma_start(x1[:, 5 * half:5 * half + 5, :],
                             x_t[5 * half:5 * half + 5].rearrange("t l d -> l t d")).then_inc(sem(f"d_x1{half}"), 16)
            sp.wait_ge(full[PLACE["C32"][0]], PLACE["C32"][1] + 1)
            sp.dma_start(w1_s[:], w_t(w1)[:, 0:2, :]).then_inc(sem("d_w1"), 16)
            sp.wait_ge(sem("s_w1"), 1)
            sp.dma_start(w1_s[:], w_t(w1)[:, 2:4, :]).then_inc(sem("d_w1"), 16)
            sp.wait_ge(sem("s_w1"), 2)
            sp.dma_start(w20_s[:], w_t(w2)[:, :, 0:P]).then_inc(sem("d_w20"), 16)
            sp.wait_ge(full[PLACE["Z72"][0]], PLACE["Z72"][1] + 1)
            sp.dma_start(w2_s[:], w_t(w2)[:, :, P:]).then_inc(sem("d_w2"), 16)
            for f in range(FB):
                sp.wait_ge(sem("s_out"), 3 * (f + 1))
                sp.dma_start(out_t[:, :, f * P:(f + 1) * P], x1[:, :, f * P:(f + 1) * P])\
                  .then_inc(sem("d_out"), 16)
            sp.wait_ge(sem("d_out"), 16 * FB)

        @block.gpsimd
        def _(pool):
            own = Own(pool, sem("own_pool"))
            pool.memset(edge[:, :, 1, :], 0).then_inc(sem("s_epad"), 1)
            c = sem("s_const")
            own.step(pool.memset(ident[:], 0.0))
            pool.affine_select(out=ident[:], in_=ident[:], compare_op=ALU.not_equal, fill=1.0, base=0,
                               pattern=[[-1, P]], channel_multiplier=1).then_inc(c, 1)
            pool.iota(win_of_lane[:], [[0, 1]], base=0, channel_multiplier=1,
                      allow_small_or_imprecise_dtypes=True).then_inc(c, 1)
            pool.iota(chunk_down[:], [[-1, NCH]], base=NCH, channel_multiplier=0,
                      allow_small_or_imprecise_dtypes=True).then_inc(c, 1)
            pool.iota(chunk_up[:], [[1, NCH]], base=1, channel_multiplier=0,
                      allow_small_or_imprecise_dtypes=True).then_inc(c, 1)
            pool.iota(iota_lane[:], [[1, P], [0, G]], base=0, channel_multiplier=0,
                      allow_small_or_imprecise_dtypes=True).then_inc(c, 1)
            pool.iota(iota_code[:], [[1, CODES]], base=0, channel_multiplier=0,
                      allow_small_or_imprecise_dtypes=True).then_inc(c, 1)
            pool.memset(code[:, NCH:], -1e6).then_inc(c, 1)
            pool.memset(slo[:, NCH:], -1.0).then_inc(c, 1)
            pool.memset(minus_half[:], -0.5).then_inc(c, 1)
            pool.memset(ones16[:], 1.0).then_inc(c, 1)
            pool.memset(zeros16[:], 0.0).then_inc(c, 1)
            pool.memset(half2[:], 0.0).then_inc(c, 1)
            pool.wait_ge(c, NCONST - 2)
            pool.memset(half2[0:DH, 0:1], 0.5).then_inc(c, 1)
            pool.wait_ge(c, NCONST - 1)
            pool.memset(half2[DH:P, 1:2], 0.5).then_inc(c, 1)
            pool.wait_ge(c, NCONST)
            pool.dma_start(proj_d[:, :, 0:DH], proj.rearrange("(a p) d -> p a d", p=P)).then_inc(sem("d_par"), 16)
            pool.dma_start(proj_d[:, :, DH:P], proj.rearrange("(a p) d -> p a d", p=P)).then_inc(sem("d_par"), 16)
            pool.dma_start(par_r[:], params).then_inc(sem("d_par"), 16)
            pool.dma_start(eps_col[:], eps.broadcast_to([P, 1])).then_inc(sem("d_par"), 16)
            pool.memset(ATlo_words[:], 0).then_inc(sem("s_atlo0"), 1)
            pool.memset(vaug[:, :, :, DH:], 1.0).then_inc(sem("s_vones"), 1)

            def inverse_root(dst_ap, var, tmp, width):
                own.step(pool.tensor_scalar(tmp, var, LN_EPS, None, ALU.add))
                own.step(pool.tensor_tensor(dst_ap, tmp, minus_half[0:var.shape[0], 0:width], ALU.pow))

            def row_scales(i, n, done):
                s, b, tmp = ln_s[:, i:i + n], ln_b[:, i:i + n], ln_tmp[:, 0, i:i + n]
                inverse_root(s, mv_row[:, i:i + n, 1], tmp, n)
                own.step(pool.tensor_tensor(ln_tmp[:, 1, i:i + n], mv_row[:, i:i + n, 0], s, ALU.mult))
                pool.tensor_scalar(b, ln_tmp[:, 1, i:i + n], -1.0, None, ALU.mult).then_inc(done, 1)

            def batch_scales(k, n, g, b, done):
                s, t = bn_s[:, k:k + n], bn_t[:, k:k + n]
                inverse_root(bn_tmp[:, 1, k:k + n], mv_f[:, k:k + n, 1], bn_tmp[:, 0, k:k + n], n)
                own.step(pool.tensor_tensor(s, bn_tmp[:, 1, k:k + n], g, ALU.mult))
                own.step(pool.tensor_tensor(bn_tmp[:, 0, k:k + n], mv_f[:, k:k + n, 0], s, ALU.mult))
                pool.tensor_tensor(t, b, bn_tmp[:, 0, k:k + n], ALU.subtract).then_inc(done, 1)

            def low_rows(i, rows, h_done, base):
                pool.wait_ge(sem(h_done), base + i + 1)
                pool.tensor_tensor(hl[:, i, :], rows[:, i % 3, :], hh[:, i, :], ALU.subtract)\
                    .then_inc(sem("s_hl"), 1)

            for pair in range(T // 2):
                pool.wait_ge(sem("s_mv"), pair + 1)
                row_scales(2 * pair, 2, sem("s_rs"))
                if pair:
                    low_rows(2 * pair - 2, hring, "s_hh", 0)
                    low_rows(2 * pair - 1, hring, "s_hh", 0)
            low_rows(T - 2, hring, "s_hh", 0)
            low_rows(T - 1, hring, "s_hh", 0)

            for slot in range(NW + 1):
                for name in (SLOTS[slot - 1] if slot else []):
                    if name in ("UK3", "UK7"):
                        h0 = 0 if name == "UK3" else 4
                        pool.wait_ge(sem("s_kmax"), 1 + h0 // 4)
                        pool.partition_all_reduce(kmaxall[:, h0:h0 + 4], kmax1[:, h0:h0 + 4], P,
                                                  bass.bass_isa.ReduceOp.max).then_inc(sem("s_kall"), 1)
                        for h in range(h0, h0 + 4):
                            pool.wait_ge(free[PLACE[f"UK{h}"][0]], PLACE[f"UK{h}"][1] + 1)
                            pool.tensor_scalar(kf[:, h % 4], kf[:, h % 4], 1.0 / 16, KEPS, ALU.mult, ALU.add)\
                                .then_inc(sem("s_kf"), 1)
                    if name[:2] == "UQ":
                        h = int(name[2])
                        pool.wait_ge(free[PLACE[name][0]], PLACE[name][1] + 1)
                        pool.tensor_scalar(qf[:, h % 2], qf[:, h % 2], 1.0 / 16, KEPS, ALU.mult, ALU.add)\
                            .then_inc(sem("s_qf"), 1)
            pool.wait_ge(sem("s_mv1"), 1)
            batch_scales(0, FB, pcol("n1g", 0, FB), pcol("n1b", 0, FB), sem("s_bn1"))

            pool.wait_ge(sem("s_wch"), 1)
            pool.tensor_tensor(wc_lo[:], wA[:], wc_hi[:].bitcast(F32), ALU.subtract).then_inc(sem("s_wc"), 1)
            n = 0
            for kind, f, ci in CONV:
                if kind == "A":
                    c0, w = COLS[ci]
                    pool.wait_ge(sem("s_agh"), n + 1)
                    pool.tensor_tensor(agg_lo[:, f, c0:c0 + w], aggf[:, n % 4, 0:w],
                                       agg_hi[:, f, c0:c0 + w].bitcast(F32), ALU.subtract)\
                        .then_inc(sem("s_agl"), 1)
                    n += 1
            pool.wait_ge(sem("s_mv2"), 1)
            batch_scales(0, FB, pcol("n2g", 0, FB), pcol("n2b", 0, FB), sem("s_bn2"))

            def add_rows(i):
                pool.tensor_tensor(x1[:, i, :], x1[:, i, :], hring1[:, i % 3, :], ALU.add).then_inc(sem("s_x1h"), 1)

            for i in range(T):
                pool.wait_ge(sem("s_mvb"), i + 1)
                row_scales(i, 1, sem("s_rsb"))
                if i:
                    low_rows(i - 1, hring1, "s_hhb", 0)
                    add_rows(i - 1)
            low_rows(T - 1, hring1, "s_hhb", 0)
            add_rows(T - 1)

            n = 0

            def low_agg1(order):
                nonlocal n
                for f, ci in order:
                    c0, w = COLS[ci]
                    pool.wait_ge(sem("s_agh1"), n + 1)
                    pool.tensor_tensor(agg_lo[:, f, c0:c0 + w], aggf[:, n % 4, 0:w],
                                       agg_hi[:, f, c0:c0 + w].bitcast(F32), ALU.subtract)\
                        .then_inc(sem("s_agl1"), 1)
                    n += 1

            low_agg1(A1_FIRST)
            for half in range(2):
                pool.wait_ge(sem("s_w1h"), half + 1)
                pool.tensor_tensor(w1_lo[:, 2 * half:2 * half + 2, :], w1_s[:],
                                   w1_hi[:, 2 * half:2 * half + 2, :].bitcast(F32), ALU.subtract)\
                    .then_inc(sem("s_w1"), 1)
            low_agg1(A1_REST)

            def low_z(b):
                pool.wait_ge(sem("s_ah"), b + 1)
                pool.tensor_tensor(a_lo[:, b, :], zr[:, b % 2, :], a_hi[:, b, :].bitcast(F32), ALU.subtract)\
                    .then_inc(sem("s_al"), 1)

            for b in range(HB):
                pool.wait_ge(sem("s_mvz"), b + 1)
                batch_scales(b, 1, pcol("g1", b), pcol("be1", b), sem("s_bnz"))
                low_z(b)
                if b == 1:
                    pool.wait_ge(sem("s_w2h"), 1)
                    pool.tensor_tensor(w20_lo[:], w20_s[:], w20_hi[:].bitcast(F32), ALU.subtract)\
                        .then_inc(sem("s_w2"), 1)
            pool.wait_ge(sem("s_w2h"), 2)
            pool.tensor_tensor(w2_lo[:], w2_s[:], w2_hi[:].bitcast(F32), ALU.subtract).then_inc(sem("s_w2"), 1)
            for f in range(FB):
                pool.wait_ge(sem("s_mvu"), f + 1)
                batch_scales(f, 1, pcol("g2", f), pcol("be2", f), sem("s_bnu"))

        @block.scalar
        def _(act):
            def copy(o, i, scale=1.0):
                return act.activation(o, i, ACT.Copy, scale=scale)

            def rows_T(i):
                ps = read_group(act, f"hT{i}")
                free_group(copy(hT[:, :, i * L:(i + 1) * L],
                                ps[:, 0:FB * L].rearrange("p (f l) -> p f l", f=FB)), f"hT{i}")

            for i in range(T):
                act.wait_ge(sem(f"d_x{i % 4}"), 16 * (i // 4 + 1))
                act.wait_ge(sem("s_rs"), i // 2 + 1)
                if i >= 3:
                    act.wait_ge(sem("s_hl"), i - 2)
                    act.wait_ge(full[PLACE[f"hT{i - 3}"][0]], PLACE[f"hT{i - 3}"][1] + 1)
                act.activation(hring[:, i % 3, :], xring[:, i % 4, :], ACT.Relu,
                               bias=ln_b[:, i:i + 1], scale=ln_s[:, i:i + 1]).then_inc(sem("s_h"), 1)
                act.activation(hh[:, i, :], xring[:, i % 4, :], ACT.Relu,
                               bias=ln_b[:, i:i + 1], scale=ln_s[:, i:i + 1]).then_inc(sem("s_hh"), 1)
                if i:
                    rows_T(i - 1)
            rows_T(T - 1)

            SCALE = float(DH) ** -0.25

            def attention(name):
                if name == "PT":
                    ps = read_group(act, name)
                    copy(projT[:], ps[:, 0:M])
                    free_group(copy(par[:], ps[:, M:M + NPAR]), name)
                elif name[0] == "V":
                    nt = int(name[1])
                    act.wait_ge(sem("s_vones"), 1)
                    ps = read_group(act, name)
                    free_group(copy(vaug[:, nt, :, 0:DH], ps[:].rearrange("p (h d) -> p h d", h=HEADS)), name)
                elif name in ("Q0", "Q1", "K0", "K1"):
                    a, f = "QK".index(name[0]), 2 * int(name[1])
                    ps = read_group(act, name)[:].rearrange("p (f n) -> p f n", f=2)
                    copy(tqk[:, a, f:f + 2, :], ps, SCALE).then_inc(sem("s_tqk"), 1)
                    free_group(act.activation(sq[:, a, f:f + 2, :], ps, ACT.Square, scale=SCALE), name)
                elif name in ("UK3", "UK7"):
                    h0 = 0 if name == "UK3" else 4
                    act.wait_ge(sem("s_nbk"), 1 + h0 // 4)
                    if h0:
                        act.wait_ge(full[PLACE["KV1"][0]], PLACE["KV1"][1] + 1)
                    else:
                        act.wait_ge(sem("s_hl"), T)
                    for h in range(h0, h0 + 4):
                        ps = read_group(act, f"UK{h}")
                        act.activation(kf[:, h % 4, 0, :], ps[:, 0:M], ACT.Exp, bias=nbk[:, h, 0:1])
                        free_group(act.activation(kf[:, h % 4, 1, :], ps[:, M:], ACT.Exp, bias=nbk[:, h, 1:2]),
                                   f"UK{h}")
                elif name[:2] == "UQ":
                    h = int(name[2])
                    act.wait_ge(sem("s_nbq"), h + 1)
                    if h >= 2:
                        act.wait_ge(full[PLACE[f"QT{h - 2}"][0]], PLACE[f"QT{h - 2}"][1] + 1)
                    ps = read_group(act, name)
                    act.activation(qf[:, h % 2, 0, :], ps[:, 0:M], ACT.Exp, bias=nbq[:, h, 0:1])
                    free_group(act.activation(qf[:, h % 2, 1, :], ps[:, M:], ACT.Exp, bias=nbq[:, h, 1:2]), name)
                elif name[:2] == "KV":
                    g = int(name[2])
                    ps = read_group(act, name)
                    free_group(copy(kv[:, 2 * g:2 * g + 2], ps[:, 0:4 * (DH + 1)]
                                    .rearrange("p (h m d) -> p h m d", h=2, m=2)), name)
                elif name[:2] == "QT":
                    h = int(name[2])
                    if h >= 2:
                        o = f"O{(h - 2) // 2}"
                        act.wait_ge(full[PLACE[o][0]], PLACE[o][1] + 1)
                    ps = read_group(act, name)
                    free_group(copy(qfT[:, h % 2], ps[:].rearrange("p (m n) -> p m n", m=2)), name)
                elif name[:2] == "AT":
                    nt = int(name[2])
                    ps = read_group(act, name)
                    free_group(copy(attnT[:, :, nt * P:(nt + 1) * P],
                                    ps[:].rearrange("p (f n) -> p f n", f=FB)), name)

            for t in range(NW):
                act.wait_ge(sem("s_win"), t + 1)
                copy(AT[:, :, t * W:(t + 1) * W],
                     banks[t % 2][0:L, 0:CODES].rearrange("p (a b) -> p a b", a=T)).then_inc(sem("s_at"), 1)
                for name in (SLOTS[t - 1] if t else []):
                    attention(name)
            for name in SLOTS[NW - 1]:
                attention(name)

            for j in range(6):
                if j == 0:
                    act.wait_ge(full[PLACE["UQ7"][0]], PLACE["UQ7"][1] + 1)
                t0 = 4 * (j % 3)
                w = min(4, T - t0) * L
                ps = read_group(act, f"degb{j}")
                free_group(copy((rdb, indb)[j // 3][:, t0 * L:t0 * L + w], ps[:, 0:w]), f"degb{j}")
            act.wait_ge(sem("d_wA"), 48)
            act.wait_ge(full[PLACE["O3"][0]], PLACE["O3"][1] + 1)
            copy(wc_hi[:], wA[:]).then_inc(sem("s_wch"), 1)
            n = 0
            for kind, f, ci in CONV:
                if kind == "A":
                    c0, w = COLS[ci]
                    act.wait_ge(sem("s_agf"), n + 1)
                    copy(agg_hi[:, f, c0:c0 + w], aggf[:, n % 4, 0:w]).then_inc(sem("s_agh"), 1)
                    n += 1

            act.wait_ge(sem("s_bn2"), 1)
            for j in range(N // PIECE):
                for f in (0, 1):
                    y = hT[:, f, j * PIECE:(j + 1) * PIECE]
                    act.activation(y, y, ACT.Identity, bias=bn_t[:, f:f + 1], scale=bn_s[:, f:f + 1])\
                       .then_inc(sem("s_yna"), 1)

            def rows_T1(i):
                ps = read_group(act, f"g{i}")
                free_group(copy(hT[:, :, i * L:(i + 1) * L],
                                ps[:, 0:FB * L].rearrange("p (f l) -> p f l", f=FB))
                           , f"g{i}")

            for i in range(T):
                act.wait_ge(sem("s_rsb"), i + 1)
                if i >= 3:
                    act.wait_ge(sem("s_x1h"), i - 2)
                    act.wait_ge(full[7], PLACE[f"g{i - 3}"][1] + 1)
                act.activation(hring1[:, i % 3, :], x1[:, i, :], ACT.Relu,
                               bias=ln_b[:, i:i + 1], scale=ln_s[:, i:i + 1]).then_inc(sem("s_hb"), 1)
                act.activation(hh[:, i, :], x1[:, i, :], ACT.Relu,
                               bias=ln_b[:, i:i + 1], scale=ln_s[:, i:i + 1]).then_inc(sem("s_hhb"), 1)
                if i:
                    rows_T1(i - 1)
            rows_T1(T - 1)

            n = 0

            def high_agg1(order):
                nonlocal n
                for f, ci in order:
                    c0, w = COLS[ci]
                    act.wait_ge(sem("s_agf1"), n + 1)
                    copy(agg_hi[:, f, c0:c0 + w], aggf[:, n % 4, 0:w]).then_inc(sem("s_agh1"), 1)
                    n += 1

            high_agg1(A1_FIRST)
            for half in range(2):
                act.wait_ge(sem("d_w1"), 16 * (half + 1))
                copy(w1_hi[:, 2 * half:2 * half + 2, :], w1_s[:]).then_inc(sem("s_w1h"), 1)
            high_agg1(A1_REST)

            def z_out(b, ci):
                c0, w = COLS[ci]
                if ci == 0 and b >= 2:
                    act.wait_ge(sem("s_al"), b - 1)
                ps = read_group(act, f"Z{b}{ci}")
                ins = act.activation(zr[:, b % 2, c0:c0 + w], ps[:, 0:w], ACT.Identity, bias=pcol("b1", b))
                free_group(ins, f"Z{b}{ci}")

            def z_norm(b):
                act.wait_ge(sem("s_bnz"), b + 1)
                act.activation(zr[:, b % 2, :], zr[:, b % 2, :], ACT.Relu,
                               bias=bn_t[:, b:b + 1], scale=bn_s[:, b:b + 1]).then_inc(sem("s_a"), 1)

            for b in range(HB):
                z_out(b, 0)
                if b:
                    z_norm(b - 1)
                z_out(b, 1)
                z_out(b, 2)
                if b == 1:
                    act.wait_ge(sem("d_w20"), 16)
                    copy(w20_hi[:], w20_s[:]).then_inc(sem("s_w2h"), 1)
            z_norm(HB - 1)
            act.wait_ge(sem("d_w2"), 16)
            copy(w2_hi[:], w2_s[:]).then_inc(sem("s_w2h"), 1)

            def u_out(f, ci):
                c0, w = COLS[ci]
                ps = read_group(act, f"U{f}{ci}")
                ins = act.activation(ur[:, f % 2, c0:c0 + w], ps[:, 0:w], ACT.Identity, bias=pcol("b2", f))
                free_group(ins, f"U{f}{ci}")

            def u_norm(f):
                act.wait_ge(sem("s_bnu"), f + 1)
                if f >= 2:
                    act.wait_ge(full[PLACE[f"out{f - 2}2"][0]], PLACE[f"out{f - 2}2"][1] + 1)
                act.activation(orr[:, f % 2, :], ur[:, f % 2, :], ACT.Relu,
                               bias=bn_t[:, f:f + 1], scale=bn_s[:, f:f + 1]).then_inc(sem("s_o"), 1)

            for f in range(FB):
                u_out(f, 0)
                if f:
                    u_norm(f - 1)
                u_out(f, 1)
                u_out(f, 2)
            u_norm(FB - 1)

        @block.vector
        def _(dve):
            own = Own(dve, sem("own_dve"))
            dve.wait_ge(sem("d_edge"), 64)
            own.mark(dve.tensor_scalar(quo[:, 0], edge[:, 0], float(WIN_MUL), None, ALU.mult))
            own.step(dve.tensor_scalar(quo[:, 1], edge[:, 1], float(TILE_MUL), None, ALU.mult))
            own.mark(dve.tensor_scalar(quo[:, 0], quo[:, 0], WIN_SHIFT, None, ALU.logical_shift_right))
            own.step(dve.tensor_scalar(quo[:, 1], quo[:, 1], TILE_SHIFT, None, ALU.logical_shift_right))
            own.mark(dve.scalar_tensor_tensor(code_r[:, 0], quo[:, 0], float(CODES - W), edge[:, 0], ALU.mult, ALU.add))
            own.mark(dve.scalar_tensor_tensor(code_r[:, 2], quo[:, 1], float(-L), edge[:, 1], ALU.mult, ALU.add))
            own.mark(dve.tensor_reduce(wm[:, 0, :], quo[:, 0], AX.X, ALU.min))
            own.step(dve.tensor_reduce(wm[:, 1, :], quo[:, 0], AX.X, ALU.max))
            dve.scalar_tensor_tensor(code_r[:, 1], quo[:, 1], float(W), code_r[:, 0], ALU.mult, ALU.add)\
               .then_inc(sem("s_prep"), 1)
            dve.wait_ge(sem("s_const"), NCONST)
            ps = read_group(dve, "codes")
            own.mark(dve.tensor_copy(code[:, 0:NCH], ps[0:CH, 0:NCH]))
            n_slo = dve.tensor_copy(slo[:, 0:NCH], ps[0:CH, NCH:2 * NCH])
            free_group(n_slo, "codes")
            ps = read_group(dve, "ranges")
            own.step(dve.tensor_scalar(sel[:, 0, :], ps[0:NW, 0:NCH], win_of_lane[:, 0:1], None, ALU.is_le))
            ins = dve.scalar_tensor_tensor(sel[:, 1, :], ps[0:NW, NCH:2 * NCH], win_of_lane[:, 0:1],
                                           sel[:, 0, :], ALU.is_ge, ALU.mult)
            free_group(ins, "ranges")
            dve.wait_ge(free[PLACE["ranges"][0]], PLACE["ranges"][1] + 1)
            own.step(dve.tensor_tensor(sel[:, 0, :], sel[:, 1, :], chunk_down[:], ALU.mult))
            own.step(dve.tensor_tensor(sel[:, 1, :], sel[:, 1, :], chunk_up[:], ALU.mult))
            dve.tensor_reduce(red[:], sel[:], AX.X, ALU.max).then_inc(sem("s_red"), 1)

            def lanes(g):
                if g == 0:
                    dve.wait_ge(free[PLACE["codes"][0]], PLACE["codes"][1] + 1)
                a = slo[:, g * G:(g + 1) * G]
                a = bass.AP(tensor=a.tensor, offset=a.offset, ap=[list(a.ap[0]), [0, P], [1, G]])
                return dve.tensor_tensor(S[:, :, g * G:(g + 1) * G], iota_lane[0:CH], a, ALU.is_equal)

            def row_stats(i):
                dve.wait_ge(sem(f"d_x{i % 4}"), 16 * (i // 4 + 1))
                own.step(dve.bn_stats(st_row[:, i % 2, :], xring[:, i % 4, :]))
                ins = dve.bn_aggr(mv_row[:, i, :], st_row[:, i % 2, :])
                if i % 2:
                    ins.then_inc(sem("s_mv"), 1)

            g = 0
            row_stats(0)
            row_stats(1)
            lanes(0)
            ps = read_group(dve, "rowranges")
            row = ps[0:1, 0:2 * NW].rearrange("p (a t) -> p a t", a=2)
            own.step(dve.tensor_scalar(rng_f[:, 0, :], row[:, 0, :], -1.0, float(NCH), ALU.mult, ALU.add))
            own.step(dve.tensor_scalar(rng_f[:, 1, :], rng_f[:, 0, :], float(NCH - 1), None, ALU.min))
            own.step(dve.scalar_tensor_tensor(rng_f[:, 2, :], rng_f[:, 1, :], 1.0, row[:, 1, :], ALU.add, ALU.max))
            own.mark(dve.tensor_copy(ranges[:, :, 0], rng_f[:, 1, :]))
            own.mark(dve.tensor_copy(ranges[:, :, 1], rng_f[:, 2, :]))
            own.step(dve.tensor_tensor(rng_f[:, 3, :], rng_f[:, 2, :], rng_f[:, 1, :], ALU.subtract))
            ins = dve.tensor_reduce(most[:], rng_f[:, 3, :], AX.X, ALU.max)
            free_group(ins, "rowranges")
            g = 1
            for i in range(2, T):
                row_stats(i)
                for _ in range(2):
                    lanes(g)
                    g += 1
            while g < (NCH + G) // G:
                ins = lanes(g)
                g += 1
            ins.then_inc(sem("s_S"), 1)

            def attention(name):
                if name == "DG":
                    ps = read_group(dve, name)
                    free_group(dve.tensor_copy(diag[:], ps[:, 0:32].rearrange("p (a h n) -> p a h n", a=2, h=HEADS)), name)
                    dve.wait_ge(free[PLACE["DG"][0]], PLACE["DG"][1] + 1)
                elif name[:2] == "UK":
                    h = int(name[2])
                    ps = read_group(dve, name)
                    own.mark(dve.tensor_reduce(kmax[:, h, :], ps[:].rearrange("p (n m) -> p n m", n=2), AX.X, ALU.max))
                    if h % 4 == 3:
                        own.after(own.n)
                        own.step(dve.tensor_tensor(kmax1[:, h - 3:h + 1], kmax[:, h - 3:h + 1, 0],
                                                   kmax[:, h - 3:h + 1, 1], ALU.max))
                        dve.sem_inc(sem("s_kmax"), 1)
                        dve.wait_ge(sem("s_kall"), h // 4 + 1)
                        for n in range(2):
                            ins = dve.scalar_tensor_tensor(nbk[:, h - 3:h + 1, n], diag[:, 1, h - 3:h + 1, n], -1.0,
                                                           kmaxall[:, h - 3:h + 1], ALU.mult, ALU.subtract)
                        ins.then_inc(sem("s_nbk"), 1)
                elif name[:2] == "UQ":
                    h = int(name[2])
                    ps = read_group(dve, name)
                    own.step(dve.tensor_reduce(qmax[:, h, :], ps[:].rearrange("p (n m) -> p n m", n=2), AX.X, ALU.max))
                    dve.scalar_tensor_tensor(nbq[:, h, :], diag[:, 0, h, :], -1.0, qmax[:, h, :],
                                             ALU.mult, ALU.subtract).then_inc(sem("s_nbq"), 1)
                elif name[0] == "O":
                    g = int(name[1])
                    ps = read_group(dve, name)[:, 0:4 * (DH + 1)].rearrange("p (h n d) -> p h n d", h=2, n=2)
                    z = zden[:, :, :].rearrange("p a (h n) -> p a h n", h=2)
                    own.step(dve.tensor_scalar(z[:, 0], ps[:, :, :, DH], KEPS, None, ALU.add))
                    own.step(dve.reciprocal(z[:, 1], z[:, 0]))
                    for h in range(2):
                        o = attn[:, :, (2 * g + h) * DH:(2 * g + h + 1) * DH]
                        zz = zden[:, 1, 2 * h:2 * h + 2].unsqueeze(2).broadcast_to([P, 2, DH])
                        ins = dve.tensor_tensor(o, ps[:, h, :, 0:DH], zz, ALU.mult)
                    free_group(ins, name)
                elif name[:2] == "WO":
                    g = 2 * int(name[2])
                    ps = read_group(dve, name)[:].rearrange("p (f n) -> p f n", f=2)
                    if g == 0:
                        own.step(dve.tensor_scalar(neg_bc[:], pcol("bc", 0, FB), -1.0, None, ALU.mult))
                    own.step(dve.tensor_copy(att255[:, g:g + 2], ps[:, :, MAXN - 1]))
                    for f in (g, g + 1):
                        dve.scalar_tensor_tensor(hT[:, f, 0:MAXN], ps[:, f - g, :], pcol("bc", f),
                                                 hT[:, f, 0:MAXN], ALU.add, ALU.add)
                        ins = own.mark(dve.tensor_scalar(hT[:, f, MAXN:], hT[:, f, MAXN:], att255[:, f:f + 1],
                                                   pcol("bc", f), ALU.add, ALU.add))
                    own.after(own.n)
                    dve.sem_inc(free[PLACE[name][0]], 1)

            def feature_stats(f, ci, ap, stat_block=None):
                return dve.bn_stats(st_f[:, stat_block if stat_block is not None else f, ci, :], ap)

            taken = dve.alloc_register("taken")
            lo_r, hi_r = dve.alloc_register("first_chunk"), dve.alloc_register("last_chunk")
            span_r, big_r = dve.alloc_register("chunks_spanned"), dve.alloc_register("exact_chunks")
            dve.reg_mov(big_r, BIG)
            dve.reg_mov(taken, 0)
            dve.wait_ge(free[PLACE["rowranges"][0]], PLACE["rowranges"][1] + 1)
            dve.wait_ge(sem("s_atlo0"), 1)
            for t in range(NW):
                dve.load([lo_r, hi_r], ranges[0:1, t, :])
                lo, hi = dve.snap(lo_r, min_val=0, max_val=NCH - 1), dve.snap(hi_r, min_val=1, max_val=NCH)
                with dve.Fori(lo, hi, G) as i:
                    for j in range(G):
                        if j % Q == 0:
                            dve.reg_add(taken, taken, Q)
                            dve.wait_ge(sem("s_slot"), dve.snap(taken, min_val=Q, max_val=1 << 20))
                        ins = dve.tensor_scalar(ring[:, j, :], iota_code[0:CH], code[:, bass.ds(i + j, 1)],
                                                float(-CODES * t), ALU.subtract, ALU.is_equal)
                        if j % Q == Q - 1:
                            ins.then_inc(sem("s_hot"), 1)
                dve.reg_sub(span_r, hi_r, lo_r)
                with dve.If_lt(big_r, span_r):
                    dve.wait_ge(sem("s_at"), t + 1)
                    dve.tensor_tensor(ATlo[:, :, t * W:(t + 1) * W],
                                      banks[t % 2][0:L, 0:CODES].rearrange("p (a b) -> p a b", a=T),
                                      AT[:, :, t * W:(t + 1) * W], ALU.subtract, saturate=False)\
                       .then_inc(sem("s_lo"), 1)
                with dve.Else():
                    dve.sem_inc(sem("s_lo"), 1)
                if 3 <= t < 3 + FB * NC:
                    f, ci = divmod(t - 3, NC)
                    if t == 3:
                        dve.wait_ge(free[PLACE["hT9"][0]], PLACE["hT9"][1] + 1)
                        dve.wait_ge(free[PLACE["hT8"][0]], PLACE["hT8"][1] + 1)
                        dve.wait_ge(free[PLACE["hT7"][0]], PLACE["hT7"][1] + 1)
                        dve.wait_ge(free[PLACE["hT6"][0]], PLACE["hT6"][1] + 1)
                    c0, w = COLS[ci]
                    own.mark(feature_stats(f, ci, hT[:, f, c0:c0 + w]))
                if t == 3 + FB * NC:
                    own.after(own.n)
                    for f in range(FB):
                        own.mark(dve.bn_aggr(mv_f[:, f, :], st_f[:, f].rearrange("p c s -> p (c s)")))
                    own.after(own.n)
                    dve.sem_inc(sem("s_mv1"), 1)
                for name in (SLOTS[t - 1] if t else []):
                    attention(name)
            for name in SLOTS[NW - 1]:
                attention(name)
            ps = read_group(dve, "deg")
            own.mark(dve.tensor_scalar(deg2[:, 1, :], ps[0:L, 0:T], 1.0, None, ALU.min))
            own.step(dve.tensor_scalar(deg2[:, 2, :], ps[0:L, 0:T], 1.0, None, ALU.max))
            ins = dve.reciprocal(deg2[:, 0, :], deg2[:, 2, :])
            free_group(ins, "deg")

            dve.wait_ge(sem("s_bn1"), 1)
            for j in range(6):
                dve.wait_ge(free[PLACE[f"degb{j}"][0]], PLACE[f"degb{j}"][1] + 1)
            pend = []
            n = 0

            def finish_agg():
                f, ci, k, mark = pend.pop(0)
                c0, w = COLS[ci]
                own.after(mark)
                if k >= 4:
                    dve.wait_ge(sem("s_agl"), k - 3)
                dve.scalar_tensor_tensor(aggf[:, k % 4, 0:w], indb[:, c0:c0 + w], bn_t[:, f:f + 1],
                                         tmpr[:, k % 2, 0:w], ALU.mult, ALU.add).then_inc(sem("s_agf"), 1)

            for kind, f, ci in CONV:
                c0, w = COLS[ci]
                name = f"{kind}{f}{ci}"
                if kind == "A":
                    ps = read_group(dve, name)
                    if n >= 2:
                        dve.wait_ge(sem("s_agf"), n - 1)
                    mark = own.mark(dve.scalar_tensor_tensor(tmpr[:, n % 2, 0:w], ps[:, 0:w], bn_s[:, f:f + 1],
                                                             rdb[:, c0:c0 + w], ALU.mult, ALU.mult))
                    pend.append((f, ci, n, mark))
                    n += 1
                    finish_agg()
                    dve.sem_inc(free[PLACE[name][0]], 1)
                else:
                    ps = read_group(dve, name)
                    ins = dve.scalar_tensor_tensor(hT[:, f, c0:c0 + w], ps[:, 0:w], neg_bc[:, f:f + 1],
                                                   hT[:, f, c0:c0 + w], ALU.max, ALU.add)
                    free_group(ins, name)
                    dve.wait_ge(free[PLACE[name][0]], PLACE[name][1] + 1)
                    own.mark(feature_stats(f, ci, hT[:, f, c0:c0 + w]))
            own.after(own.n)
            for f in range(FB):
                own.mark(dve.bn_aggr(mv_f[:, f, :], st_f[:, f].rearrange("p c s -> p (c s)")))
            own.after(own.n)
            dve.sem_inc(sem("s_mv2"), 1)

            dve.wait_ge(sem("s_bn2"), 1)
            for j in range(N // PIECE):
                for f in (2, 3):
                    y = hT[:, f, j * PIECE:(j + 1) * PIECE]
                    dve.tensor_scalar(y, y, bn_s[:, f:f + 1], bn_t[:, f:f + 1], ALU.mult, ALU.add)\
                       .then_inc(sem("s_ynd"), 1)
            dve.wait_ge(sem("d_par"), 64)
            own.mark(dve.tensor_scalar(eps1[:], eps_col[:], 1.0, None, ALU.add))
            for i in range(T):
                if i % 5 == 0:
                    dve.wait_ge(sem(f"d_x1{i // 5}"), 16)
                ps = read_group(dve, f"x{i}")
                ins = dve.tensor_tensor(x1[:, i, :], ps[0:L, :], x1[:, i, :], ALU.add)
                free_group(ins, f"x{i}")
                dve.wait_ge(free[6], PLACE[f"x{i}"][1] + 1)
                own.step(dve.bn_stats(st_row[:, i % 2, :], x1[:, i, :]))
                dve.bn_aggr(mv_row[:, i, :], st_row[:, i % 2, :]).then_inc(sem("s_mvb"), 1)

            own.after(own.n)
            for k, (f, ci) in enumerate(A1_FIRST + A1_REST):
                c0, w = COLS[ci]
                if k == 0:
                    dve.wait_ge(free[7], PLACE["g9"][1] + 1)
                ps = read_group(dve, f"B{f}{ci}")
                if k >= 4:
                    dve.wait_ge(sem("s_agl1"), k - 3)
                ins = dve.scalar_tensor_tensor(aggf[:, k % 4, 0:w], hT[:, f, c0:c0 + w], eps1[:, 0:1],
                                               ps[:, 0:w], ALU.mult, ALU.add).then_inc(sem("s_agf1"), 1)
                dve.wait_ge(sem("s_agf1"), k + 1)
                dve.sem_inc(free[PLACE[f"B{f}{ci}"][0]], 1)

            def z_stats(b, ci):
                c0, w = COLS[ci]
                bank, turn = PLACE[f"Z{b}{ci}"]
                dve.wait_ge(free[bank], turn + 1)
                own.mark(feature_stats(b, ci, zr[:, b % 2, c0:c0 + w]))

            def z_high(b):
                dve.wait_ge(sem("s_a"), b + 1)
                dve.tensor_copy(a_hi[:, b, :], zr[:, b % 2, :]).then_inc(sem("s_ah"), 1)

            for b in range(HB):
                z_stats(b, 0)
                if b:
                    z_high(b - 1)
                z_stats(b, 1)
                z_stats(b, 2)
                own.after(own.n)
                dve.bn_aggr(mv_f[:, b, :], st_f[:, b].rearrange("p c s -> p (c s)")).then_inc(sem("s_mvz"), 1)
            z_high(HB - 1)

            dve.wait_ge(sem("s_x1h"), T)

            def out_add(f):
                for j, (t0, t1) in enumerate(OUT_TILES):
                    ps = read_group(dve, f"out{f}{j}")
                    o = x1[:, t0:t1, f * P:(f + 1) * P]
                    ins = dve.tensor_tensor(o, ps[0:L, 0:(t1 - t0) * P].rearrange("p (t d) -> p t d", d=P), o, ALU.add)
                    own.step(ins)
                    dve.sem_inc(free[PLACE[f"out{f}{j}"][0]], 1)
                    dve.sem_inc(sem("s_out"), 1)

            for f in range(FB):
                for ci in range(NC):
                    c0, w = COLS[ci]
                    bank, turn = PLACE[f"U{f}{ci}"]
                    dve.wait_ge(free[bank], turn + 1)
                    own.mark(feature_stats(f, ci, ur[:, f % 2, c0:c0 + w]))
                    if f and ci == 0:
                        out_add(f - 1)
                own.after(own.n)
                dve.bn_aggr(mv_f[:, f, :], st_f[:, f].rearrange("p c s -> p (c s)")).then_inc(sem("s_mvu"), 1)
            out_add(FB - 1)

        @block.tensor
        def _(pe):
            def mm(o, l, r, start, stop):
                return pe.matmul(o, l, r, start=start, stop=stop, skip_group_check=True)

            pe.wait_ge(sem("s_const"), NCONST)
            pe.wait_ge(sem("s_prep"), 1)
            rest = NCH - P
            ps = open_group(pe, "codes")
            for a, k in enumerate((1, 2)):
                pe.transpose(ps[0:CH, a * NCH:a * NCH + P], code_r[:, k, 0, :], ident[:])
                ins = pe.transpose(ps[0:CH, a * NCH + P:(a + 1) * NCH], code_r[0:rest, k, 1, :],
                                   ident[0:rest, 0:rest])
            close_group(ins, "codes")
            ps = open_group(pe, "ranges")
            for a in range(2):
                mm(ps[0:NW, a * NCH:a * NCH + P], wm[:, a, 0:1].broadcast_to([P, NW]), ident[:], True, True)
                ins = mm(ps[0:NW, a * NCH + P:(a + 1) * NCH], wm[0:rest, a, 1:2].broadcast_to([rest, NW]),
                         ident[0:rest, 0:rest], True, True)
            close_group(ins, "ranges")
            pe.wait_ge(sem("s_red"), 1)
            ps = open_group(pe, "rowranges")
            for a in range(2):
                ins = mm(ps[0:1, a * NW:(a + 1) * NW], red[:, a:a + 1], ident[0:NW, 0:NW], True, True)
            close_group(ins, "rowranges")

            def turn_rows(i, rows, h_done, name):
                pe.wait_ge(sem(h_done), i + 1)
                ps = open_group(pe, name)
                for f in range(FB):
                    ins = pe.transpose(ps[:, f * L:(f + 1) * L], rows[:, i % 3, f * P:(f + 1) * P], ident[0:L, 0:L])
                close_group(ins, name)

            for i in range(T):
                turn_rows(i, hring, "s_h", f"hT{i}")

            hT_ready = [False]

            def released(name):
                bank, turn = PLACE[name]
                pe.wait_ge(free[bank], turn + 1)

            def attention(name):
                if name[0] in "VQK" and name[:2] not in ("KV", "QT") and not hT_ready[0]:
                    for i in range(3):
                        released(f"hT{i}")
                    hT_ready[0] = True
                if name == "PT":
                    pe.wait_ge(sem("d_par"), 64)
                    ps = open_group(pe, name)
                    for a in range(2):
                        pe.transpose(ps[:, a * P:(a + 1) * P], proj_d[:, a, :], ident[:])
                    ins = pe.transpose(ps[:, M:M + NPAR], par_r[:], ident[0:NPAR, 0:NPAR])
                elif name[0] == "V":
                    nt = int(name[1])
                    pe.wait_ge(sem("d_wA"), 16)
                    ps = open_group(pe, name)
                    for k in range(FB):
                        ins = mm(ps[:], hT[:, k, nt * P:(nt + 1) * P], wA[:, k, :], k == 0, k == FB - 1)
                elif name in ("Q0", "Q1", "K0", "K1"):
                    w, d, n = (wB, "d_wB", 16) if name[0] == "Q" else (wA, "d_wA", 32)
                    pe.wait_ge(sem(d), n)
                    ps = open_group(pe, name)
                    for j in range(2):
                        f = 2 * int(name[1]) + j
                        for k in range(FB):
                            ins = mm(ps[:, j * MAXN:(j + 1) * MAXN], w[:, k, f * P:(f + 1) * P], hT[:, k, 0:MAXN],
                                     k == 0, k == FB - 1)
                elif name == "DG":
                    for q in ("Q0", "Q1", "K0", "K1"):
                        released(q)
                    ps = open_group(pe, name)
                    for a in range(2):
                        for f in range(FB):
                            for n in range(2):
                                c = 16 * a + 4 * f + n
                                ins = mm(ps[:, c:c + 3:2], sq[:, a, f, n * P:(n + 1) * P], half2[:], True, True)
                elif name[:2] in ("UQ", "UK"):
                    a, h = "QK".index(name[1]), int(name[2])
                    ps = open_group(pe, name)
                    p0 = DH * (h % 2)
                    for n in range(2):
                        ins = mm(ps[:, n * M:(n + 1) * M], tqk[p0:p0 + DH, a, h // 2, n * P:(n + 1) * P],
                                 projT[p0:p0 + DH, :], True, True)
                elif name[:2] == "KV":
                    g = int(name[2])
                    pe.wait_ge(sem("s_kf"), 2 * g + 2)
                    ps = open_group(pe, name)[:, 0:4 * (DH + 1)].rearrange("p (h m d) -> p h m d", h=2, m=2)
                    for j in range(2):
                        h = 2 * g + j
                        for m in range(2):
                            for n in range(2):
                                ins = mm(ps[:, j, m, :], kf[:, h % 4, n, m * P:(m + 1) * P], vaug[:, n, h, :],
                                         n == 0, n == 1)
                elif name[:2] == "QT":
                    h = int(name[2])
                    pe.wait_ge(sem("s_qf"), h + 1)
                    ps = open_group(pe, name)[:].rearrange("p (m n) -> p m n", m=2)
                    for m in range(2):
                        for n in range(2):
                            ins = pe.transpose(ps[:, m, n * P:(n + 1) * P], qf[:, h % 2, n, m * P:(m + 1) * P], ident[:])
                elif name[0] == "O":
                    g = int(name[1])
                    released(f"KV{g}")
                    released(f"QT{2 * g}")
                    released(f"QT{2 * g + 1}")
                    ps = open_group(pe, name)[:, 0:4 * (DH + 1)].rearrange("p (h n d) -> p h n d", h=2, n=2)
                    for j in range(2):
                        h = 2 * g + j
                        for n in range(2):
                            for m in range(2):
                                ins = mm(ps[:, j, n, :], qfT[:, h % 2, m, n * P:(n + 1) * P], kv[:, h, m, :],
                                         m == 0, m == 1)
                elif name[:2] == "AT":
                    nt = int(name[2])
                    released("O3")
                    ps = open_group(pe, name)
                    for f in range(FB):
                        ins = pe.transpose(ps[:, f * P:(f + 1) * P], attn[:, nt, f * P:(f + 1) * P], ident[:])
                elif name[:2] == "WO":
                    pe.wait_ge(sem("d_wB"), 32)
                    released("AT0")
                    released("AT1")
                    ps = open_group(pe, name)
                    for j in range(2):
                        f = 2 * int(name[2]) + j
                        for k in range(FB):
                            ins = mm(ps[:, j * MAXN:(j + 1) * MAXN], wB[:, k, f * P:(f + 1) * P], attnT[:, k, :],
                                     k == 0, k == FB - 1)
                close_group(ins, name)

            seen = pe.alloc_register("seen")
            lo_r, hi_r = pe.alloc_register("first_chunk_pe"), pe.alloc_register("last_chunk_pe")
            most_r, big_r = pe.alloc_register("most_chunks"), pe.alloc_register("exact_chunks_pe")
            pe.reg_mov(big_r, BIG)
            pe.reg_mov(seen, 0)
            pe.wait_ge(free[PLACE["rowranges"][0]], PLACE["rowranges"][1] + 1)
            pe.load([most_r], most[0:1, 0:1])
            pe.wait_ge(sem("s_S"), 1)
            pe.sem_inc(sem("s_slot"), G)
            for t in range(NW):
                pe.load([lo_r, hi_r], ranges[0:1, t, :])
                lo, hi = pe.snap(lo_r, min_val=0, max_val=NCH - 1), pe.snap(hi_r, min_val=1, max_val=NCH)
                if t >= 2:
                    pe.wait_ge(sem("s_at"), t - 1)
                    pe.wait_ge(sem("s_lo"), t - 1)
                ps = banks[t % 2]
                mm(ps[:, 0:CODES], ones16[0:CH, :], zeros16[0:CH, :], True, False)
                with pe.Fori(lo, hi, G) as i:
                    for j in range(G):
                        if j % Q == 0:
                            pe.reg_add(seen, seen, 1)
                            pe.wait_ge(sem("s_hot"), pe.snap(seen, min_val=1, max_val=1 << 20))
                        ins = mm(ps[:, 0:CODES], S[:, :, bass.ds(i + j, 1)].rearrange("e l c -> e (l c)"),
                                 ring[:, j, :], False, False)
                        if j % Q == Q - 1:
                            ins.then_inc(sem("s_slot"), Q)
                mm(ps[:, 0:1], ones16[0:CH, :], zeros16[0:CH, 0:1], False, True).then_inc(sem("s_win"), 1)
                for name in SLOTS[t]:
                    attention(name)

            pe.wait_ge(sem("s_at"), NW)
            pe.wait_ge(sem("s_lo"), NW)

            def accumulate(ps, pairs, extra, finish):
                mm(ps, *pairs[0], True, False)
                with pe.If_lt(big_r, most_r):
                    for l, r in extra:
                        mm(ps, l, r, False, False)
                pe.end_ifs() if finish else None
                for n, (l, r) in enumerate(pairs[1:]):
                    ins = mm(ps, l, r, False, n == len(pairs) - 2)
                return ins

            ps = open_group(pe, "deg")
            for i in range(T):
                cols = slice(i * L, (i + 1) * L)
                ins = accumulate(ps[0:L, i:i + 1], [(AT[:, k, cols], ones16[0:L, 0:1]) for k in range(T)],
                                 [(ATlo[:, k, cols], ones16[0:L, 0:1]) for k in range(T)], True)
            close_group(ins, "deg")
            released("deg")
            for j in range(6):
                ps = open_group(pe, f"degb{j}")
                t0 = 4 * (j % 3)
                for i in range(t0, min(t0 + 4, T)):
                    ins = mm(ps[:, (i - t0) * L:(i - t0 + 1) * L],
                             deg2[:, j // 3, i:i + 1].broadcast_to([L, P]), ident[0:L, 0:L], True, True)
                close_group(ins, f"degb{j}")

            pe.wait_ge(sem("s_hl"), T)

            def split3(ps, w, wts, acts, ks, order_wait=None):
                (w_hi, w_lo), (x_hi, x_lo) = wts, acts
                n = 0
                for k in ks:
                    if order_wait:
                        order_wait(k)
                    for a, b in ((w_hi, x_hi), (w_hi, x_lo), (w_lo, x_hi)):
                        ins = mm(ps[:, 0:w], a(k), b(k), n == 0, n == 3 * len(ks) - 1)
                        n += 1
                return ins

            for kind, f, ci in CONV:
                c0, w = COLS[ci]
                name = f"{kind}{f}{ci}"
                if kind == "A":
                    ps = open_group(pe, name)
                    fs = slice(f * P, (f + 1) * P)
                    ins = accumulate(ps[:, 0:w],
                                     [(h[:, k, fs], AT[:, k, c0:c0 + w]) for k in range(T) for h in (hh, hl)],
                                     [(h[:, k, fs], ATlo[:, k, c0:c0 + w]) for k in range(T) for h in (hh, hl)], True)
                else:
                    pe.wait_ge(sem("s_wc"), 1)
                    pe.wait_ge(sem("s_agl"), FB * (ci + 1))
                    ps = open_group(pe, name)
                    fs = slice(f * P, (f + 1) * P)
                    ins = split3(ps, w, (lambda k: wc_hi[:, k, fs], lambda k: wc_lo[:, k, fs]),
                                 (lambda k: agg_hi[:, k, c0:c0 + w], lambda k: agg_lo[:, k, c0:c0 + w]), range(FB))
                close_group(ins, name)

            first = A1_FIRST

            def agg1_rows(k):
                pe.wait_ge(sem("s_hl"), T + k + 1)
                for f, ci in first:
                    c0, w = COLS[ci]
                    name = f"B{f}{ci}"
                    ps = open_group(pe, name) if k == 0 else banks[PLACE[name][0]]
                    fs = slice(f * P, (f + 1) * P)
                    mm(ps[:, 0:w], hh[:, k, fs], AT[:, k, c0:c0 + w], k == 0, False)
                    ins = mm(ps[:, 0:w], hl[:, k, fs], AT[:, k, c0:c0 + w], False, k == T - 1)
                    if k == T - 1:
                        close_group(ins, name)

            def agg1_extra():
                with pe.If_lt(big_r, most_r):
                    for f, ci in first:
                        c0, w = COLS[ci]
                        fs = slice(f * P, (f + 1) * P)
                        for k in range(T - 1):
                            for h in (hh, hl):
                                mm(banks[PLACE[f"B{f}{ci}"][0]][:, 0:w], h[:, k, fs], ATlo[:, k, c0:c0 + w], False, False)
                pe.end_ifs()

            def agg1_extra_last():
                pe.wait_ge(sem("s_hl"), 2 * T)
                with pe.If_lt(big_r, most_r):
                    for f, ci in first:
                        c0, w = COLS[ci]
                        fs = slice(f * P, (f + 1) * P)
                        for h in (hh, hl):
                            mm(banks[PLACE[f"B{f}{ci}"][0]][:, 0:w], h[:, T - 1, fs], ATlo[:, T - 1, c0:c0 + w],
                               False, False)
                pe.end_ifs()

            for i in range(T):
                pe.wait_ge(sem("s_yna"), 2 * (i // 2 + 1))
                pe.wait_ge(sem("s_ynd"), 2 * (i // 2 + 1))
                ps = open_group(pe, f"x{i}")
                for f in range(FB):
                    ins = pe.transpose(ps[0:L, f * P:(f + 1) * P], hT[:, f, i * L:(i + 1) * L], ident[:])
                close_group(ins, f"x{i}")
                if i >= 1:
                    turn_rows(i - 1, hring1, "s_hb", f"g{i - 1}")
                if i >= 2:
                    agg1_rows(i - 2)
            turn_rows(T - 1, hring1, "s_hb", f"g{T - 1}")
            agg1_rows(T - 2)
            agg1_extra()
            agg1_extra_last()
            agg1_rows(T - 1)
            for f, ci in A1_REST:
                c0, w = COLS[ci]
                ps = open_group(pe, f"B{f}{ci}")
                fs = slice(f * P, (f + 1) * P)
                ins = accumulate(ps[:, 0:w],
                                 [(h[:, k, fs], AT[:, k, c0:c0 + w]) for k in range(T) for h in (hh, hl)],
                                 [(h[:, k, fs], ATlo[:, k, c0:c0 + w]) for k in range(T) for h in (hh, hl)], True)
                close_group(ins, f"B{f}{ci}")

            pe.wait_ge(sem("s_w1"), 2)
            for b in range(HB):
                for ci in range(NC):
                    c0, w = COLS[ci]
                    if b == 0:
                        pe.wait_ge(sem("s_agl1"), len(A1_FIRST) + 2 * (ci + 1))
                    ps = open_group(pe, f"Z{b}{ci}")
                    bs = slice(b * P, (b + 1) * P)
                    ins = split3(ps, w, (lambda k: w1_hi[:, k, bs], lambda k: w1_lo[:, k, bs]),
                                 (lambda k: agg_hi[:, k, c0:c0 + w], lambda k: agg_lo[:, k, c0:c0 + w]), range(FB))
                    close_group(ins, f"Z{b}{ci}")

            def out_rows(f):
                pe.wait_ge(sem("s_o"), f + 1)
                for j, (t0, t1) in enumerate(OUT_TILES):
                    ps = open_group(pe, f"out{f}{j}")
                    for i in range(t0, t1):
                        ins = pe.transpose(ps[0:L, (i - t0) * P:(i - t0 + 1) * P],
                                           orr[:, f % 2, i * L:(i + 1) * L], ident[:])
                    close_group(ins, f"out{f}{j}")

            for f in range(FB):
                pe.wait_ge(sem("s_w2"), 1 if f == 0 else 2)
                for ci in range(NC):
                    c0, w = COLS[ci]
                    ps = open_group(pe, f"U{f}{ci}")
                    if f == 0:
                        wts = (lambda k: w20_hi[:, k, :], lambda k: w20_lo[:, k, :])
                    else:
                        fs = slice((f - 1) * P, f * P)
                        wts = (lambda k: w2_hi[:, k, fs], lambda k: w2_lo[:, k, fs])
                    wait = (lambda k: pe.wait_ge(sem("s_al"), k + 1)) if f == 0 and ci == 0 else None
                    ins = split3(ps, w, wts, (lambda k: a_hi[:, k, c0:c0 + w], lambda k: a_lo[:, k, c0:c0 + w]),
                                 range(HB), wait)
                    close_group(ins, f"U{f}{ci}")
                    if f and ci == 0:
                        out_rows(f - 1)
            out_rows(FB - 1)


def kernel(**inputs):
    import numpy as _np
    import concourse.bacc as _bacc
    from concourse import mybir as _mybir
    from concourse.bass_utils import run_bass_kernel_spmd as _run

    def get(name):
        return _np.ascontiguousarray(inputs[name])

    p0, p1 = "L0_gnn_", "L1_gnn_"
    names = [p0 + "norm1_g", p0 + "norm1_b", p0 + "norm2_g", p0 + "norm2_b", p0 + "b_conv",
             p1 + "b1", p1 + "g1", p1 + "be1", p1 + "b2", p1 + "g2", p1 + "be2"]
    arrays = {
        "x": get("x"), "src": get("src"), "dst": get("dst"),
        "params": _np.concatenate([get(n) for n in names]).reshape(NPAR, P),
        "eps": get(p1 + "eps").reshape(1, 1),
        "w_conv": get(p0 + "W_conv"), "wq": get(p0 + "Wq"), "wk": get(p0 + "Wk"), "wv": get(p0 + "Wv"),
        "wo": get(p0 + "Wo"), "proj": get(p0 + "proj"), "w1": get(p1 + "W1"), "w2": get(p1 + "W2"),
    }
    nc = _bacc.Bacc("TRN2", target_bir_lowering=False, num_devices=1)
    args = {k: nc.dram_tensor(k, a.shape, _mybir.dt.from_np(a.dtype), kind="ExternalInput").ap()
            for k, a in arrays.items()}
    o = nc.dram_tensor("out", (N, D), _mybir.dt.float32, kind="ExternalOutput").ap()
    gnn_kernel(nc, out=o, **args)
    r = _run(nc, [arrays], core_ids=[0])
    return r.results[0]["out"]
```

```python
from contextlib import ExitStack

import concourse.bass as bass
from concourse import mybir

F32 = mybir.dt.float32
F32R = mybir.dt.float32r
F16 = mybir.dt.float16
F8 = mybir.dt.float8e4
I32 = mybir.dt.int32
U8 = mybir.dt.uint8
ALU = mybir.AluOpType
ACT = mybir.ActivationFunctionType
AX = mybir.AxisListType

P = 128
KIB = 1024

N, D, HID, E = 1250, 512, 1024, 20000
HEADS, DH, M, MAXN = 8, 64, 256, 256
LN_EPS = BN_EPS = 1e-5
KEPS = 1e-6

T = 10
L = N // T
FB = D // P
HB = HID // P
CH = 125
NCH = E // CH
G = 8
Q = 4
W = 50
NW = N // W
CODES = T * W
BIG = 16
COLS = [(0, 418), (418, 416), (834, 416)]
NC = len(COLS)
PIECE = 2 * L
WIN_SHIFT, WIN_MUL = 16, 1311
TILE_SHIFT, TILE_MUL = 17, 1049
assert all(d * WIN_MUL >> WIN_SHIFT == d // W and d * TILE_MUL >> TILE_SHIFT == d // L for d in range(N))
assert NCH == 160 and L * T == N and W * NW == N and CODES <= 512 and BIG * CH <= 2048

PARAMS = [("n1g", FB), ("n1b", FB), ("n2g", FB), ("n2b", FB), ("bc", FB),
          ("b1", HB), ("g1", HB), ("be1", HB), ("b2", FB), ("g2", FB), ("be2", FB)]
NPAR = sum(n for _, n in PARAMS)
PAR0 = {}
for _n, _k in PARAMS:
    PAR0[_n] = sum(k for _, k in PARAMS[:len(PAR0)])

SLOTS = [s.split() for s in (
    "hT0 hT1 SPAN", "hT2 hT3 PT", "hT4 hT5 V0", "hT6 hT7 V1", "hT8 hT9 K0", "K1", "Q0", "Q1 UK0", "UK1 DG", "UK2 UK3",
    "UQ0 UQ1", "KV0 KV1", "QT0 QT1", "UK4 UK5", "UK6 UK7 UQ2", "O0 UQ3", "KV2 KV3 QT2", "QT3 UQ4", "O1 UQ5",
    "QT4 UQ6", "QT5 UQ7", "O2", "QT6 QT7 D0", "O3 D1", "AT0 AT1", "D2", "WO0 WO1", "")]
STATS_AT = 4
ATT = [name for slot in SLOTS for name in slot]
assert len(SLOTS) >= NW


def conv_order():
    out = [("A", f, 0) for f in range(FB)]
    for c in range(NC):
        if c + 1 < NC:
            out += [("A", f, c + 1) for f in range(FB)]
        out += [("C", f, c) for f in range(FB)]
    return out


CONV = conv_order()
A1_FIRST = [(f, c) for f in (0, 1) for c in range(NC)]
A1_REST = [(f, c) for c in range(NC) for f in (2, 3)]


def plan_banks():
    place, used = {}, [0] * 8

    def take(name, bank):
        place[name] = (bank, used[bank])
        used[bank] += 1

    take("codes", 2)
    take("ranges", 3)
    for n, name in enumerate(ATT):
        take(name, 2 + n % 6)
    for n, (kind, f, c) in enumerate(CONV):
        take(f"{kind}{f}{c}", n % 8)
    for n, (f, c) in enumerate(A1_FIRST):
        take(f"B{f}{c}", n)
    for i in range(T):
        take(f"x{i}", 6)
        take(f"g{i}", 7)
    for n, (f, c) in enumerate(A1_REST):
        take(f"B{f}{c}", n)
    n = 6
    for b in range(HB):
        for c in range(NC):
            take(f"Z{b}{c}", n % 8)
            n += 1
    n = 0
    for f in range(FB):
        for c in range(NC):
            take(f"U{f}{c}", n % 6)
            n += 1
        for j in range(3):
            take(f"out{f}{j}", 6 + (3 * f + j) % 2)
    return place


PLACE = plan_banks()
W1_AT = (3, 7)
OUT_TILES = [(0, 4), (4, 8), (8, 10)]


class Own:

    def __init__(self, eng, sem):
        self.eng, self.sem, self.n = eng, sem, 0

    def mark(self, ins):
        self.n += 1
        ins.then_inc(self.sem, 1)
        return self.n

    def after(self, n):
        self.eng.wait_ge(self.sem, n)

    def step(self, ins):
        self.after(self.mark(ins))


def gnn_kernel(nc, x, src, dst, params, eps, w_conv, wq, wk, wv, wo, proj, w1, w2, out):
    with ExitStack() as ctx:
        sems = {}

        def sem(name):
            if name not in sems:
                sems[name] = ctx.enter_context(nc.semaphore(name))
            return sems[name]

        def place(name, shape, dt, kib):
            pad = nc.sbuf_tensor(name + "_at", [P, int(kib * KIB)], U8)
            pad.__enter__()
            it = nc.sbuf_tensor(name, shape, dt)
            t = it.__enter__()
            it.__exit__(None, None, None)
            pad.__exit__(None, None, None)
            return t

        iota_code = place("iota_code", [P, CODES], F16, 0.25)
        iota_lane = place("iota_lane", [P, P, G], F16, 1.25)
        ones16 = place("ones16", [P, P], F16, 3.25)
        zeros16 = place("zeros16", [P, 1], F16, 3.5)
        ident = place("ident", [P, P], F32, 4.5)
        chunk_down = place("chunk_down", [NW, NCH], F32, 5)
        chunk_up = place("chunk_up", [NW, NCH], F32, 5.625)
        par = place("par", [P, NPAR], F32, 6.25)
        half2 = place("half2", [P, 2], F32, 6.5)
        minus_half = place("minus_half", [P, T], F32, 6.53125)
        win_of_lane = place("win_of_lane", [NW, 1], F32, 6.59375)
        eps1 = place("eps1", [P, 1], F32, 6.625)
        eps_col = place("eps_col", [P, 1], F32, 6.65625)
        tables = place("tables", [P, 1], F32, 7.625)
        ranges = place("ranges", [NW, 2], I32, 6.6875)
        most = place("most", [1, 1], I32, 6.90625)
        neg_bc = place("neg_bc", [P, FB], F32, 6.9375)
        rng_f = place("rng_f", [NW, 4], F32, 7)
        red = place("red", [NW, 2], F32, 7.40625)
        wm = place("wm", [P, 2, 2], F32, 7.4375)
        st_row = place("st_row", [L, 2, 6], F32, 7.46875)
        att255 = place("att255", [P, FB], F32, 7.5625)
        st_f = place("st_f", [P, HB, NC, 6], F32, 86.25)
        mv_f = place("mv_f", [P, HB, 2], F32, 86.84375)
        mv_row = place("mv_row", [L, T, 2], F32, 86.90625)
        bn_tmp = place("bn_tmp", [P, 2, HB], F32, 87)
        bn_s = place("bn_s", [P, HB], F32, 87.09375)
        bn_t = place("bn_t", [P, HB], F32, 87.125)
        ln_tmp = place("ln_tmp", [L, 2, T], F32, 87.15625)
        ln_s = place("ln_s", [L, T], F32, 87.25)
        ln_b = place("ln_b", [L, T], F32, 87.3125)
        kmax = place("kmax", [P, HEADS, 2], F32, 87.375)
        kmax1 = place("kmax1", [P, HEADS], F32, 87.4375)
        kmaxall = place("kmaxall", [P, HEADS], F32, 87.46875)
        nbk = place("nbk", [P, HEADS, 2], F32, 87.5)
        nbq = place("nbq", [P, HEADS, 2], F32, 87.5625)
        qmax = place("qmax", [P, HEADS, 2], F32, 87.625)
        zden = place("zden", [P, 2, 4], F32, 87.6875)
        diag = place("diag", [P, 2, HEADS, 2], F32, 87.75)
        AT = place("AT", [L, T, N], F16, 8)
        ATlo_all = place("ATlo", [L, T * N], F8, 32.5)
        ATlo = ATlo_all[:].rearrange("p (t n) -> p t n", t=T)
        hh = place("hh", [L, T, D], F16, 45)
        hl = place("hl", [L, T, D], F16, 55)
        hT = place("hT", [P, FB, N], F32, 65)
        S = place("S", [CH, P, NCH + G], F16, 88)
        ring = place("ring", [CH, G, CODES], F16, 130)
        tqk = place("tqk", [P, 2, FB, MAXN], F32, 138)
        sq = place("sq", [P, 2, FB, MAXN], F32, 146)
        wA = place("wA", [P, FB, D], F32, 154)
        wB = place("wB", [P, FB, D], F32, 162)
        vaug = place("vaug", [P, 2, HEADS, DH + 1], F32, 170)
        attn = place("attn", [P, 2, D], F32, 174.25)
        attnT = place("attnT", [P, FB, MAXN], F32, 178.25)
        HR = 7
        hring = place("hring", [L, HR, D], F32, 182.25)
        x_in = place("x_in", [L, 8, D], F32, 138)
        x_in2 = place("x_in2", [L, 2, D], F32, 174.25)

        def x_tile(i):
            return x_in[:, i, :] if i < 8 else x_in2[:, i - 8, :]

        edge = place("edge", [P, 2, 2, CH], I32, 196.25)
        quo = place("quo", [P, 2, 2, CH], I32, 198.25)
        code_r = place("code_r", [P, 3, 2, CH], F32, 200.25)
        kf = place("kf", [P, 4, 2, M], F32, 182.25)
        qf = place("qf", [P, 2, 2, M], F32, 190.25)
        qfT = place("qfT", [P, 2, 2, MAXN], F32, 194.25)
        kv = place("kv", [P, HEADS, 2, DH + 1], F32, 198.25)
        projT = place("projT", [P, M], F32, 203.25)
        proj_d = place("proj_d", [P, 2, P], F32, 204.25)
        par_r = place("par_r", [NPAR, P], F32, 205.25)
        code = place("code", [CH, NCH + G], F32, 205.75)
        slo = place("slo", [CH, NCH + G], F16, 206.4375)
        sel = place("sel", [NW, 2, NCH], F32, 85)
        agg_hi = place("agg_hi", [P, FB, N], F32R, 88)
        agg_lo = place("agg_lo", [P, FB, N], F32R, 107.5625)
        tmpr = place("tmpr", [P, 2, COLS[0][1]], F32, 127.25)
        aggf = place("aggf", [P, 4, COLS[0][1]], F32, 130.75)
        rdb = place("rdb", [P, N], F32, 138)
        indb = place("indb", [P, N], F32, 143)
        wc_hi = place("wc_hi", [P, FB, D], F32R, 182.25)
        wc_lo = place("wc_lo", [P, FB, D], F32R, 190.25)
        x1 = place("x1", [L, T, D], F32, 154)
        w1_hi = place("w1_hi", [P, FB, HID], F32R, 138)
        w1_lo = place("w1_lo", [P, FB, HID], F32R, 174)
        w1_s = place("w1_s", [P, 2, HID], F32, 190)
        hring1 = place("hring1", [L, 3, D], F32, 198.25)
        a_hi = place("a_hi", [P, HB, N], F32R, 8)
        a_lo = place("a_lo", [P, HB, N], F32R, 47.125)
        zr = place("zr", [P, 2, N], F32, 127.25)
        w2_s, w2_hi, w2_lo = ([place(f"w2_{kind}{f}", [P, HB, P], F32 if kind == "s" else F32R, at)
                               for f, at in enumerate(ats)]
                              for kind, ats in (("s", (190, 202, 96, 108)), ("hi", (194, 88, 100, 112)),
                                                ("lo", (198, 92, 104, 116))))
        ur = place("ur", [P, 2, N], F32, 138)
        orr = place("orr", [P, 2, N], F32, 174)

        banks = [ctx.enter_context(nc.psum_tensor(f"bank{i}", [P, 512], F32)) for i in range(8)]

        full = [sem(f"full{i}") for i in range(8)]
        free = [sem(f"free{i}") for i in range(8)]

        def open_group(eng, name):
            bank, turn = PLACE[name]
            if turn:
                eng.wait_ge(free[bank], turn)
            return banks[bank]

        def close_group(ins, name):
            ins.then_inc(full[PLACE[name][0]], 1)

        def read_group(eng, name):
            bank, turn = PLACE[name]
            eng.wait_ge(full[bank], turn + 1)
            return banks[bank]

        def free_group(ins, name):
            ins.then_inc(free[PLACE[name][0]], 1)

        def pcol(name, k=0, n=1):
            return par[:, PAR0[name] + k:PAR0[name] + k + n]

        x_t = x.rearrange("(t l) d -> t l d", l=L)
        out_t = out.rearrange("(t l) d -> l t d", l=L)
        dst_t, src_t = (a.rearrange("(c e) -> c e", e=CH) for a in (dst, src))

        def w_t(w):
            return w.rearrange("(k p) n -> p k n", p=P)

        NCONST = 14
        block = ctx.enter_context(nc.Block())

        @block.sync
        def _(sp):
            for a, d in enumerate((dst_t, src_t)):
                sp.dma_start(edge[:, a, 0, :], d[0:P, :]).then_inc(sem("d_edge"), 16)
            sp.wait_ge(sem("s_epad"), 1)
            for a, d in enumerate((dst_t, src_t)):
                sp.dma_start(edge[0:NCH - P, a, 1, :], d[P:NCH, :]).then_inc(sem("d_edge"), 16)
            for i in range(0, T, 2):
                sp.dma_start(x_in[:, i:i + 2, :] if i < 8 else x_in2[:], x_t[i:i + 2].rearrange("t l d -> l t d"))\
                  .then_inc(sem(f"d_x{i // 2}"), 16)
            sp.dma_start(wA[:], w_t(wv)).then_inc(sem("d_wA"), 16)
            sp.dma_start(wB[:], w_t(wk)).then_inc(sem("d_wB"), 16)
            sp.wait_ge(full[PLACE["V1"][0]], PLACE["V1"][1] + 1)
            sp.dma_start(wA[:], w_t(wq)).then_inc(sem("d_wA"), 16)
            sp.wait_ge(full[PLACE["K1"][0]], PLACE["K1"][1] + 1)
            sp.dma_start(wB[:], w_t(wo)).then_inc(sem("d_wB"), 16)
            sp.wait_ge(full[PLACE["Q1"][0]], PLACE["Q1"][1] + 1)
            sp.dma_start(wA[:], w_t(w_conv)).then_inc(sem("d_wA"), 16)
            sp.wait_ge(full[PLACE["WO1"][0]], PLACE["WO1"][1] + 1)
            sp.wait_ge(sem("s_wc"), 1)
            for half in range(2):
                sp.dma_start(x1[:, 5 * half:5 * half + 5, :],
                             x_t[5 * half:5 * half + 5].rearrange("t l d -> l t d")).then_inc(sem(f"d_x1{half}"), 16)
            sp.wait_ge(full[PLACE["C32"][0]], PLACE["C32"][1] + 1)
            sp.dma_start(w1_s[:], w_t(w1)[:, 0:2, :]).then_inc(sem("d_w1"), 16)
            sp.wait_ge(sem("s_w1"), 1)
            sp.dma_start(w1_s[:], w_t(w1)[:, 2:4, :]).then_inc(sem("d_w1"), 16)
            sp.wait_ge(sem("s_w1"), 2)
            for f in range(FB):
                if f == 1:
                    sp.wait_ge(sem("s_x1h"), T)
                    sp.wait_ge(sem("s_hlb"), T)
                    sp.wait_ge(full[PLACE["g9"][0]], PLACE["g9"][1] + 1)
                if f == 2:
                    sp.wait_ge(full[PLACE["Z72"][0]], PLACE["Z72"][1] + 1)
                sp.dma_start(w2_s[f][:], w_t(w2)[:, :, f * P:(f + 1) * P]).then_inc(sem(f"d_w2{f}"), 16)
            for f in range(FB - 1):
                sp.wait_ge(sem("s_out"), 3 * (f + 1))
                sp.dma_start(out_t[:, :, f * P:(f + 1) * P], x1[:, :, f * P:(f + 1) * P])\
                  .then_inc(sem("d_out"), 16)
            for j, (t0, t1) in enumerate(OUT_TILES):
                sp.wait_ge(sem("s_out"), 3 * (FB - 1) + j + 1)
                sp.dma_start(out_t[:, t0:t1, (FB - 1) * P:], x1[:, t0:t1, (FB - 1) * P:]).then_inc(sem("d_out"), 16)
            sp.wait_ge(sem("d_out"), 16 * (FB - 1 + len(OUT_TILES)))

        @block.gpsimd
        def _(pool):
            own = Own(pool, sem("own_pool"))
            pool.memset(edge[:, :, 1, :], 0).then_inc(sem("s_epad"), 1)
            c = sem("s_const")
            own.step(pool.memset(ident[:], 0.0))
            pool.affine_select(out=ident[:], in_=ident[:], compare_op=ALU.not_equal, fill=1.0, base=0,
                               pattern=[[-1, P]], channel_multiplier=1).then_inc(c, 1)
            pool.iota(win_of_lane[:], [[0, 1]], base=0, channel_multiplier=1,
                      allow_small_or_imprecise_dtypes=True).then_inc(c, 1)
            pool.iota(chunk_down[:], [[-1, NCH]], base=NCH, channel_multiplier=0,
                      allow_small_or_imprecise_dtypes=True).then_inc(c, 1)
            pool.iota(chunk_up[:], [[1, NCH]], base=1, channel_multiplier=0,
                      allow_small_or_imprecise_dtypes=True).then_inc(c, 1)
            pool.iota(iota_lane[:], [[1, P], [0, G]], base=0, channel_multiplier=0,
                      allow_small_or_imprecise_dtypes=True).then_inc(c, 1)
            pool.iota(iota_code[:], [[1, CODES]], base=0, channel_multiplier=0,
                      allow_small_or_imprecise_dtypes=True).then_inc(c, 1)
            pool.memset(code[:, NCH:], -1e6).then_inc(c, 1)
            pool.memset(slo[:, NCH:], -1.0).then_inc(c, 1)
            pool.memset(minus_half[:], -0.5).then_inc(c, 1)
            pool.memset(ones16[:], 1.0).then_inc(c, 1)
            pool.memset(zeros16[:], 0.0).then_inc(c, 1)
            pool.memset(half2[:], 0.0).then_inc(c, 1)
            pool.wait_ge(c, NCONST - 2)
            pool.memset(half2[0:DH, 0:1], 0.5).then_inc(c, 1)
            pool.wait_ge(c, NCONST - 1)
            pool.memset(half2[DH:P, 1:2], 0.5).then_inc(c, 1)
            pool.wait_ge(c, NCONST)
            pool.memset(vaug[:, :, :, DH:], 1.0).then_inc(sem("s_vones"), 1)

            def inverse_root(dst_ap, var, tmp, width):
                own.step(pool.tensor_scalar(tmp, var, LN_EPS, None, ALU.add))
                own.step(pool.tensor_tensor(dst_ap, tmp, minus_half[0:var.shape[0], 0:width], ALU.pow))

            def row_scales(i, n, done):
                s, b, tmp = ln_s[:, i:i + n], ln_b[:, i:i + n], ln_tmp[:, 0, i:i + n]
                inverse_root(s, mv_row[:, i:i + n, 1], tmp, n)
                own.step(pool.tensor_tensor(ln_tmp[:, 1, i:i + n], mv_row[:, i:i + n, 0], s, ALU.mult))
                pool.tensor_scalar(b, ln_tmp[:, 1, i:i + n], -1.0, None, ALU.mult).then_inc(done, 1)

            def batch_scales(k, n, g, b, done):
                s, t = bn_s[:, k:k + n], bn_t[:, k:k + n]
                inverse_root(bn_tmp[:, 1, k:k + n], mv_f[:, k:k + n, 1], bn_tmp[:, 0, k:k + n], n)
                own.step(pool.tensor_tensor(s, bn_tmp[:, 1, k:k + n], g, ALU.mult))
                own.step(pool.tensor_tensor(bn_tmp[:, 0, k:k + n], mv_f[:, k:k + n, 0], s, ALU.mult))
                pool.tensor_tensor(t, b, bn_tmp[:, 0, k:k + n], ALU.subtract).then_inc(done, 1)

            def low_rows(i):
                pool.wait_ge(sem("s_hh"), i + 1)
                pool.tensor_tensor(hl[:, i, :], hring[:, i % HR, :], hh[:, i, :], ALU.subtract)\
                    .then_inc(sem("s_hl"), 1)

            for pair in range(T // 2):
                pool.wait_ge(sem("s_mv"), pair + 1)
                row_scales(2 * pair, 2, sem("s_rs"))
                if pair == 0:
                    pool.memset(ATlo_all[:].bitcast(I32), 0).then_inc(sem("s_atlo0"), 1)
                if pair:
                    low_rows(2 * pair - 2)
                    low_rows(2 * pair - 1)
            low_rows(T - 2)
            low_rows(T - 1)

            for slot in range(len(SLOTS) + 1):
                for name in (SLOTS[slot - 1] if slot else []):
                    if name in ("UK3", "UK7"):
                        h0 = 0 if name == "UK3" else 4
                        pool.wait_ge(sem("s_kmax"), 1 + h0 // 4)
                        own.step(pool.partition_all_reduce(kmaxall[:, h0:h0 + 4], kmax1[:, h0:h0 + 4], P,
                                                           bass.bass_isa.ReduceOp.max))
                        b = nbk[:, h0:h0 + 4, :]
                        own.step(pool.tensor_tensor(b, diag[:, 1, h0:h0 + 4, :],
                                                    kmaxall[:, h0:h0 + 4].unsqueeze(2).broadcast_to([P, 4, 2]), ALU.add))
                        pool.tensor_scalar(b, b, -1.0, None, ALU.mult).then_inc(sem("s_nbk"), 1)
                        for h in range(h0, h0 + 4):
                            pool.wait_ge(free[PLACE[f"UK{h}"][0]], PLACE[f"UK{h}"][1] + 1)
                            pool.tensor_scalar(kf[:, h % 4], kf[:, h % 4], 1.0 / 16, KEPS, ALU.mult, ALU.add)\
                                .then_inc(sem("s_kf"), 1)
                    if name[:2] == "UQ":
                        h = int(name[2])
                        pool.wait_ge(free[PLACE[name][0]], PLACE[name][1] + 1)
                        pool.tensor_scalar(qf[:, h % 2], qf[:, h % 2], 1.0 / 16, KEPS, ALU.mult, ALU.add)\
                            .then_inc(sem("s_qf"), 1)
            pool.wait_ge(sem("s_mv1"), 1)
            batch_scales(0, FB, pcol("n1g", 0, FB), pcol("n1b", 0, FB), sem("s_bn1"))

            pool.wait_ge(sem("s_wch"), 1)
            pool.tensor_tensor(wc_lo[:], wA[:], wc_hi[:].bitcast(F32), ALU.subtract).then_inc(sem("s_wc"), 1)
            n = 0
            for kind, f, ci in CONV:
                if kind == "A":
                    c0, w = COLS[ci]
                    pool.wait_ge(sem("s_agh"), n + 1)
                    pool.tensor_tensor(agg_lo[:, f, c0:c0 + w], aggf[:, n % 4, 0:w],
                                       agg_hi[:, f, c0:c0 + w].bitcast(F32), ALU.subtract)\
                        .then_inc(sem("s_agl"), 1)
                    n += 1
            pool.wait_ge(sem("s_mv2"), 1)
            batch_scales(0, FB, pcol("n2g", 0, FB), pcol("n2b", 0, FB), sem("s_bn2"))

            def add_rows(i):
                pool.wait_ge(sem("s_hb"), i + 1)
                pool.wait_ge(sem("s_hhb"), i + 1)
                pool.tensor_tensor(x1[:, i, :], x1[:, i, :], hring1[:, i % 3, :], ALU.add).then_inc(sem("s_x1h"), 1)

            for i in range(T):
                pool.wait_ge(sem("s_mvb"), i + 1)
                row_scales(i, 1, sem("s_rsb"))
                if i:
                    add_rows(i - 1)
            add_rows(T - 1)

            n = 0

            def low_agg1(order):
                nonlocal n
                for f, ci in order:
                    c0, w = COLS[ci]
                    pool.wait_ge(sem("s_agh1"), n + 1)
                    pool.tensor_tensor(agg_lo[:, f, c0:c0 + w], aggf[:, n % 4, 0:w],
                                       agg_hi[:, f, c0:c0 + w].bitcast(F32), ALU.subtract)\
                        .then_inc(sem("s_agl1"), 1)
                    n += 1

            low_agg1(A1_FIRST)
            low_agg1(A1_REST)

            def low_z(b):
                pool.wait_ge(sem("s_ah"), b + 1)
                pool.tensor_tensor(a_lo[:, b, :], zr[:, b % 2, :], a_hi[:, b, :].bitcast(F32), ALU.subtract)\
                    .then_inc(sem("s_al"), 1)

            for b in range(HB):
                pool.wait_ge(sem("s_mvz"), b + 1)
                batch_scales(b, 1, pcol("g1", b), pcol("be1", b), sem("s_bnz"))
                if b < HB - 1:
                    low_z(b)
            for f in range(FB):
                pool.wait_ge(sem("s_mvu"), f + 1)
                batch_scales(f, 1, pcol("g2", f), pcol("be2", f), sem("s_bnu"))

        @block.scalar
        def _(act):
            act.wait_ge(sem("s_const"), NCONST)
            act.activation(tables[:], half2[:, 0:1], ACT.Copy)
            act.dma_start(par_r[:], params).then_inc(sem("d_par"), 16)
            for a in range(2):
                act.dma_start(proj_d[:, :, a * DH:(a + 1) * DH], proj.rearrange("(a p) d -> p a d", p=P))\
                   .then_inc(sem("d_par"), 16)
            act.dma_start(eps_col[:], eps.broadcast_to([P, 1])).then_inc(sem("d_par"), 16)

            def copy(o, i, scale=1.0):
                return act.activation(o, i, ACT.Copy, scale=scale)

            def rows_T(i):
                ps = read_group(act, f"hT{i}")
                free_group(copy(hT[:, :, i * L:(i + 1) * L],
                                ps[:, 0:FB * L].rearrange("p (f l) -> p f l", f=FB)), f"hT{i}")

            def rows(i):
                act.wait_ge(sem(f"d_x{i // 2}"), 16)
                act.wait_ge(sem("s_rs"), i // 2 + 1)
                if i >= HR:
                    act.wait_ge(sem("s_hl"), i - HR + 1)
                    act.wait_ge(full[PLACE[f"hT{i - HR}"][0]], PLACE[f"hT{i - HR}"][1] + 1)
                act.activation(hring[:, i % HR, :], x_tile(i), ACT.Relu,
                               bias=ln_b[:, i:i + 1], scale=ln_s[:, i:i + 1]).then_inc(sem("s_h"), 1)
                act.activation(hh[:, i, :], x_tile(i), ACT.Relu,
                               bias=ln_b[:, i:i + 1], scale=ln_s[:, i:i + 1]).then_inc(sem("s_hh"), 1)

            SCALE = float(DH) ** -0.25

            def attention(name):
                if name[:2] == "hT":
                    rows_T(int(name[2]))
                elif name == "PT":
                    ps = read_group(act, name)
                    copy(projT[:], ps[:, 0:M])
                    free_group(copy(par[:], ps[:, M:M + NPAR]), name)
                elif name[0] == "V":
                    nt = int(name[1])
                    act.wait_ge(sem("s_vones"), 1)
                    ps = read_group(act, name)
                    free_group(copy(vaug[:, nt, :, 0:DH], ps[:].rearrange("p (h d) -> p h d", h=HEADS)), name)
                elif name in ("Q0", "Q1", "K0", "K1"):
                    a, f = "QK".index(name[0]), 2 * int(name[1])
                    ps = read_group(act, name)[:].rearrange("p (f n) -> p f n", f=2)
                    copy(tqk[:, a, f:f + 2, :], ps, SCALE).then_inc(sem("s_tqk"), 1)
                    free_group(act.activation(sq[:, a, f:f + 2, :], ps, ACT.Square, scale=SCALE), name)
                elif name in ("UK3", "UK7"):
                    h0 = 0 if name == "UK3" else 4
                    act.wait_ge(sem("s_nbk"), 1 + h0 // 4)
                    if h0:
                        act.wait_ge(full[PLACE["KV1"][0]], PLACE["KV1"][1] + 1)
                    else:
                        act.wait_ge(sem("s_hl"), T)
                    for h in range(h0, h0 + 4):
                        ps = read_group(act, f"UK{h}")
                        act.activation(kf[:, h % 4, 0, :], ps[:, 0:M], ACT.Exp, bias=nbk[:, h, 0:1])
                        free_group(act.activation(kf[:, h % 4, 1, :], ps[:, M:], ACT.Exp, bias=nbk[:, h, 1:2]),
                                   f"UK{h}")
                elif name[:2] == "UQ":
                    h = int(name[2])
                    act.wait_ge(sem("s_nbq"), h + 1)
                    if h >= 2:
                        act.wait_ge(full[PLACE[f"QT{h - 2}"][0]], PLACE[f"QT{h - 2}"][1] + 1)
                    ps = read_group(act, name)
                    act.activation(qf[:, h % 2, 0, :], ps[:, 0:M], ACT.Exp, bias=nbq[:, h, 0:1])
                    free_group(act.activation(qf[:, h % 2, 1, :], ps[:, M:], ACT.Exp, bias=nbq[:, h, 1:2]), name)
                elif name[:2] == "KV":
                    g = int(name[2])
                    ps = read_group(act, name)
                    free_group(copy(kv[:, 2 * g:2 * g + 2], ps[:, 0:4 * (DH + 1)]
                                    .rearrange("p (h m d) -> p h m d", h=2, m=2)), name)
                elif name[:2] == "QT":
                    h = int(name[2])
                    if h >= 2:
                        o = f"O{(h - 2) // 2}"
                        act.wait_ge(full[PLACE[o][0]], PLACE[o][1] + 1)
                    ps = read_group(act, name)
                    free_group(copy(qfT[:, h % 2], ps[:].rearrange("p (m n) -> p m n", m=2)), name)
                elif name[:2] == "AT":
                    nt = int(name[2])
                    ps = read_group(act, name)
                    free_group(copy(attnT[:, :, nt * P:(nt + 1) * P],
                                    ps[:].rearrange("p (f n) -> p f n", f=FB)), name)

            for t in range(len(SLOTS)):
                for name in SLOTS[t]:
                    if name[:2] == "hT":
                        rows(int(name[2]))
                for name in (SLOTS[t - 1] if t else []):
                    attention(name)
                if t < NW:
                    act.wait_ge(sem("s_win"), t + 1)
                    copy(AT[:, :, t * W:(t + 1) * W],
                         banks[t % 2][0:L, 0:CODES].rearrange("p (a b) -> p a b", a=T)).then_inc(sem("s_at"), 1)

            act.wait_ge(sem("d_wA"), 48)
            act.wait_ge(full[PLACE["O3"][0]], PLACE["O3"][1] + 1)
            copy(wc_hi[:], wA[:]).then_inc(sem("s_wch"), 1)
            n = 0
            for kind, f, ci in CONV:
                if kind == "A":
                    c0, w = COLS[ci]
                    act.wait_ge(sem("s_agf"), n + 1)
                    copy(agg_hi[:, f, c0:c0 + w], aggf[:, n % 4, 0:w]).then_inc(sem("s_agh"), 1)
                    n += 1

            act.wait_ge(sem("s_bn2"), 1)
            for j in range(N // PIECE):
                for f in (0, 1):
                    y = hT[:, f, j * PIECE:(j + 1) * PIECE]
                    act.activation(y, y, ACT.Identity, bias=bn_t[:, f:f + 1], scale=bn_s[:, f:f + 1])\
                       .then_inc(sem("s_yna"), 1)

            def rows_T1(i):
                ps = read_group(act, f"g{i}")
                free_group(copy(hT[:, :, i * L:(i + 1) * L],
                                ps[:, 0:FB * L].rearrange("p (f l) -> p f l", f=FB)), f"g{i}")

            for i in range(T):
                act.wait_ge(sem("s_rsb"), i + 1)
                if i >= 3:
                    act.wait_ge(sem("s_x1h"), i - 2)
                    act.wait_ge(sem("s_hlb"), i - 2)
                    act.wait_ge(full[7], PLACE[f"g{i - 3}"][1] + 1)
                act.activation(hring1[:, i % 3, :], x1[:, i, :], ACT.Relu,
                               bias=ln_b[:, i:i + 1], scale=ln_s[:, i:i + 1]).then_inc(sem("s_hb"), 1)
                act.activation(hh[:, i, :], x1[:, i, :], ACT.Relu,
                               bias=ln_b[:, i:i + 1], scale=ln_s[:, i:i + 1]).then_inc(sem("s_hhb"), 1)
                if i:
                    rows_T1(i - 1)
                if i in W1_AT:
                    half = W1_AT.index(i)
                    act.wait_ge(sem("d_w1"), 16 * (half + 1))
                    copy(w1_hi[:, 2 * half:2 * half + 2, :], w1_s[:]).then_inc(sem("s_w1h"), 1)
            rows_T1(T - 1)

            n = 0

            def high_agg1(order):
                nonlocal n
                for f, ci in order:
                    c0, w = COLS[ci]
                    act.wait_ge(sem("s_agf1"), n + 1)
                    copy(agg_hi[:, f, c0:c0 + w], aggf[:, n % 4, 0:w]).then_inc(sem("s_agh1"), 1)
                    n += 1

            high_agg1(A1_FIRST)
            high_agg1(A1_REST)

            def z_out(b, ci):
                c0, w = COLS[ci]
                if ci == 0 and b >= 2:
                    act.wait_ge(sem("s_al"), b - 1)
                ps = read_group(act, f"Z{b}{ci}")
                ins = act.activation(zr[:, b % 2, c0:c0 + w], ps[:, 0:w], ACT.Identity, bias=pcol("b1", b))
                free_group(ins, f"Z{b}{ci}")

            def z_norm(b):
                act.wait_ge(sem("s_bnz"), b + 1)
                for c0, w in [(0, N)] if b < HB - 1 else COLS:
                    z = zr[:, b % 2, c0:c0 + w]
                    act.activation(z, z, ACT.Relu, bias=bn_t[:, b:b + 1], scale=bn_s[:, b:b + 1])\
                       .then_inc(sem("s_a"), 1)

            def w2_high(f):
                act.wait_ge(sem(f"d_w2{f}"), 16)
                if f == 1:
                    act.wait_ge(full[PLACE["Z72"][0]], PLACE["Z72"][1] + 1)
                copy(w2_hi[f][:], w2_s[f][:]).then_inc(sem("s_w2h"), 1)

            for b in range(HB):
                z_out(b, 0)
                if b:
                    z_norm(b - 1)
                z_out(b, 1)
                z_out(b, 2)
                if b == 1:
                    w2_high(0)
            z_norm(HB - 1)
            w2_high(1)

            def u_out(f, ci):
                c0, w = COLS[ci]
                ps = read_group(act, f"U{f}{ci}")
                ins = act.activation(ur[:, f % 2, c0:c0 + w], ps[:, 0:w], ACT.Identity, bias=pcol("b2", f))
                free_group(ins, f"U{f}{ci}")

            def u_norm(f):
                act.wait_ge(sem("s_bnu"), f + 1)
                if f >= 2:
                    act.wait_ge(full[PLACE[f"out{f - 2}2"][0]], PLACE[f"out{f - 2}2"][1] + 1)
                for t0, t1 in OUT_TILES:
                    act.activation(orr[:, f % 2, t0 * L:t1 * L], ur[:, f % 2, t0 * L:t1 * L], ACT.Relu,
                                   bias=bn_t[:, f:f + 1], scale=bn_s[:, f:f + 1]).then_inc(sem("s_o"), 1)

            for f in range(FB):
                u_out(f, 0)
                if f:
                    u_norm(f - 1)
                u_out(f, 1)
                u_out(f, 2)
                if f == 0:
                    w2_high(2)
                    w2_high(3)
            u_norm(FB - 1)

        @block.vector
        def _(dve):
            own = Own(dve, sem("own_dve"))
            dve.wait_ge(sem("d_edge"), 64)
            own.mark(dve.tensor_scalar(quo[:, 0], edge[:, 0], float(WIN_MUL), None, ALU.mult))
            own.step(dve.tensor_scalar(quo[:, 1], edge[:, 1], float(TILE_MUL), None, ALU.mult))
            own.mark(dve.tensor_scalar(quo[:, 0], quo[:, 0], WIN_SHIFT, None, ALU.logical_shift_right))
            own.step(dve.tensor_scalar(quo[:, 1], quo[:, 1], TILE_SHIFT, None, ALU.logical_shift_right))
            own.mark(dve.scalar_tensor_tensor(code_r[:, 0], quo[:, 0], float(CODES - W), edge[:, 0], ALU.mult, ALU.add))
            own.mark(dve.scalar_tensor_tensor(code_r[:, 2], quo[:, 1], float(-L), edge[:, 1], ALU.mult, ALU.add))
            own.mark(dve.tensor_reduce(wm[:, 0, :], quo[:, 0], AX.X, ALU.min))
            own.step(dve.tensor_reduce(wm[:, 1, :], quo[:, 0], AX.X, ALU.max))
            dve.scalar_tensor_tensor(code_r[:, 1], quo[:, 1], float(W), code_r[:, 0], ALU.mult, ALU.add)\
               .then_inc(sem("s_prep"), 1)
            def row_stats(i):
                dve.wait_ge(sem(f"d_x{i // 2}"), 16)
                own.step(dve.bn_stats(st_row[:, i % 2, :], x_tile(i)))
                ins = dve.bn_aggr(mv_row[:, i, :], st_row[:, i % 2, :])
                if i % 2:
                    ins.then_inc(sem("s_mv"), 1)

            row_stats(0)
            row_stats(1)
            dve.wait_ge(sem("s_const"), NCONST)
            ps = read_group(dve, "codes")
            own.mark(dve.tensor_copy(code[:, 0:NCH], ps[0:CH, 0:NCH]))
            n_slo = dve.tensor_copy(slo[:, 0:NCH], ps[0:CH, NCH:2 * NCH])
            free_group(n_slo, "codes")
            ps = read_group(dve, "ranges")
            own.step(dve.tensor_scalar(sel[:, 0, :], ps[0:NW, 0:NCH], win_of_lane[:, 0:1], None, ALU.is_le))
            ins = dve.scalar_tensor_tensor(sel[:, 1, :], ps[0:NW, NCH:2 * NCH], win_of_lane[:, 0:1],
                                           sel[:, 0, :], ALU.is_ge, ALU.mult)
            free_group(ins, "ranges")
            dve.wait_ge(free[PLACE["ranges"][0]], PLACE["ranges"][1] + 1)
            own.step(dve.tensor_tensor(sel[:, 0, :], sel[:, 1, :], chunk_down[:], ALU.mult))
            own.step(dve.tensor_tensor(sel[:, 1, :], sel[:, 1, :], chunk_up[:], ALU.mult))
            own.step(dve.tensor_reduce(red[:], sel[:], AX.X, ALU.max))
            own.step(dve.tensor_scalar(rng_f[:, 0:1], red[:, 0:1], -1.0, float(NCH), ALU.mult, ALU.add))
            own.step(dve.tensor_scalar(rng_f[:, 1:2], rng_f[:, 0:1], float(NCH - 1), None, ALU.min))
            own.step(dve.scalar_tensor_tensor(rng_f[:, 2:3], rng_f[:, 1:2], 1.0, red[:, 1:2], ALU.add, ALU.max))
            own.step(dve.tensor_copy(ranges[:], rng_f[:, 1:3]))
            dve.sem_inc(sem("s_ranges"), 1)
            dve.tensor_tensor(rng_f[:, 3:4], rng_f[:, 2:3], rng_f[:, 1:2], ALU.subtract).then_inc(sem("s_span"), 1)

            def lanes(c):
                a = slo[:, bass.ds(c, G)].unsqueeze(1).broadcast_to([CH, P, G])
                dve.tensor_tensor(S[:, :, bass.ds(c, G)], iota_lane[0:CH], a, ALU.is_equal)

            dve.wait_ge(free[PLACE["codes"][0]], PLACE["codes"][1] + 1)
            lanes(0)
            lanes(G)

            def span():
                ps = read_group(dve, "SPAN")
                free_group(dve.tensor_reduce(most[:], ps[0:1, 0:NW], AX.X, ALU.max), "SPAN")

            def attention(name):
                if name == "SPAN":
                    span()
                elif name == "DG":
                    ps = read_group(dve, name)
                    free_group(dve.tensor_copy(diag[:], ps[:, 0:32].rearrange("p (a h n) -> p a h n", a=2, h=HEADS)), name)
                    dve.wait_ge(free[PLACE["DG"][0]], PLACE["DG"][1] + 1)
                elif name[:2] == "UK":
                    h = int(name[2])
                    ps = read_group(dve, name)
                    own.mark(dve.tensor_reduce(kmax[:, h, :], ps[:].rearrange("p (n m) -> p n m", n=2), AX.X, ALU.max))
                    if h % 4 == 3:
                        own.after(own.n)
                        own.step(dve.tensor_tensor(kmax1[:, h - 3:h + 1], kmax[:, h - 3:h + 1, 0],
                                                   kmax[:, h - 3:h + 1, 1], ALU.max))
                        dve.sem_inc(sem("s_kmax"), 1)
                elif name[:2] == "UQ":
                    h = int(name[2])
                    ps = read_group(dve, name)
                    own.step(dve.tensor_reduce(qmax[:, h, :], ps[:].rearrange("p (n m) -> p n m", n=2), AX.X, ALU.max))
                    dve.scalar_tensor_tensor(nbq[:, h, :], diag[:, 0, h, :], -1.0, qmax[:, h, :],
                                             ALU.mult, ALU.subtract).then_inc(sem("s_nbq"), 1)
                elif name[0] == "O":
                    g = int(name[1])
                    ps = read_group(dve, name)[:, 0:4 * (DH + 1)].rearrange("p (h n d) -> p h n d", h=2, n=2)
                    z = zden[:, :, :].rearrange("p a (h n) -> p a h n", h=2)
                    own.step(dve.tensor_scalar(z[:, 0], ps[:, :, :, DH], KEPS, None, ALU.add))
                    own.step(dve.reciprocal(z[:, 1], z[:, 0]))
                    for h in range(2):
                        o = attn[:, :, (2 * g + h) * DH:(2 * g + h + 1) * DH]
                        zz = zden[:, 1, 2 * h:2 * h + 2].unsqueeze(2).broadcast_to([P, 2, DH])
                        ins = dve.tensor_tensor(o, ps[:, h, :, 0:DH], zz, ALU.mult)
                    free_group(ins, name)
                elif name[0] == "D":
                    c0, w = COLS[int(name[1])]
                    if name == "D0":
                        dve.wait_ge(full[PLACE["UQ7"][0]], PLACE["UQ7"][1] + 1)
                    ps = read_group(dve, name)
                    own.mark(dve.tensor_scalar(indb[:, c0:c0 + w], ps[:, 0:w], 1.0, None, ALU.min))
                    own.step(dve.tensor_scalar(rdb[:, c0:c0 + w], ps[:, 0:w], 1.0, None, ALU.max))
                    n_deg[0] = own.mark(dve.reciprocal(rdb[:, c0:c0 + w], rdb[:, c0:c0 + w]))
                    dve.sem_inc(free[PLACE[name][0]], 1)
                elif name[:2] == "WO":
                    g = 2 * int(name[2])
                    ps = read_group(dve, name)[:].rearrange("p (f n) -> p f n", f=2)
                    if g == 0:
                        own.step(dve.tensor_scalar(neg_bc[:], pcol("bc", 0, FB), -1.0, None, ALU.mult))
                    own.step(dve.tensor_copy(att255[:, g:g + 2], ps[:, :, MAXN - 1]))
                    for f in (g, g + 1):
                        dve.scalar_tensor_tensor(hT[:, f, 0:MAXN], ps[:, f - g, :], pcol("bc", f),
                                                 hT[:, f, 0:MAXN], ALU.add, ALU.add)
                        ins = own.mark(dve.tensor_scalar(hT[:, f, MAXN:], hT[:, f, MAXN:], att255[:, f:f + 1],
                                                   pcol("bc", f), ALU.add, ALU.add))
                    own.after(own.n)
                    dve.sem_inc(free[PLACE[name][0]], 1)

            n_deg = [0]

            def feature_stats(f, ci, ap):
                return dve.bn_stats(st_f[:, f, ci, :], ap)

            taken = dve.alloc_register("taken")
            lo_r, hi_r = dve.alloc_register("first_chunk"), dve.alloc_register("last_chunk")
            span_r, big_r = dve.alloc_register("chunks_spanned"), dve.alloc_register("exact_chunks")
            dve.reg_mov(big_r, BIG)
            dve.wait_ge(sem("s_ranges"), 1)
            dve.reg_mov(taken, 0)
            built = dve.alloc_register("lanes_built")
            need_r = dve.alloc_register("lanes_needed")
            dve.reg_mov(built, 2 * G)

            def low_counts(t):
                if t == 1:
                    dve.wait_ge(sem("s_atlo0"), 1)
                with dve.If_lt(big_r, span_r):
                    if t < 1:
                        dve.wait_ge(sem("s_atlo0"), 1)
                    dve.wait_ge(sem("s_at"), t + 1)
                    dve.tensor_tensor(ATlo[:, :, t * W:(t + 1) * W],
                                      banks[t % 2][0:L, 0:CODES].rearrange("p (a b) -> p a b", a=T),
                                      AT[:, :, t * W:(t + 1) * W], ALU.subtract, saturate=False)\
                       .then_inc(sem("s_lo"), 1)
                with dve.Else():
                    dve.sem_inc(sem("s_lo"), 1)

            for t in range(NW):
                dve.load([lo_r, hi_r], ranges[t:t + 1, :])
                lo, hi = dve.snap(lo_r, min_val=0, max_val=NCH - 1), dve.snap(hi_r, min_val=1, max_val=NCH)
                dve.reg_add(need_r, hi_r, G - 1)
                with dve.If_lt(built, need_r):
                    with dve.Fori(dve.snap(built, min_val=0, max_val=NCH), dve.snap(need_r, min_val=G, max_val=NCH + G - 1),
                                  G) as c:
                        c = nc.s_assert_within(c, 0, NCH, skip_runtime_bounds_check_because=
                                               "a multiple of G below NCH + G - 1, and G divides NCH")
                        lanes(c)
                        dve.reg_add(built, built, G)
                dve.end_ifs()
                with dve.Fori(lo, hi, G) as i:
                    for j in range(G):
                        if j % Q == 0:
                            dve.reg_add(taken, taken, Q)
                            dve.wait_ge(sem("s_slot"), dve.snap(taken, min_val=Q, max_val=1 << 20))
                        ins = dve.tensor_scalar(ring[:, j, :], iota_code[0:CH], code[:, bass.ds(i + j, 1)],
                                                float(-CODES * t), ALU.subtract, ALU.is_equal)
                        if j % Q == Q - 1:
                            ins.then_inc(sem("s_hot"), 1)
                if t:
                    low_counts(t - 1)
                dve.reg_sub(span_r, hi_r, lo_r)
                for i in (2 + 2 * t, 3 + 2 * t):
                    if i < T:
                        row_stats(i)
                for n in (2 * (t - STATS_AT), 2 * (t - STATS_AT) + 1):
                    if not 0 <= n < FB * NC:
                        continue
                    f, ci = divmod(n, NC)
                    if n == 0:
                        for i in range(T):
                            dve.wait_ge(free[PLACE[f"hT{i}"][0]], PLACE[f"hT{i}"][1] + 1)
                    c0, w = COLS[ci]
                    own.mark(feature_stats(f, ci, hT[:, f, c0:c0 + w]))
                if t == STATS_AT + FB * NC // 2:
                    own.after(own.n)
                    for f in range(FB):
                        own.mark(dve.bn_aggr(mv_f[:, f, :], st_f[:, f].rearrange("p c s -> p (c s)")))
                    own.after(own.n)
                    dve.sem_inc(sem("s_mv1"), 1)
                for name in (SLOTS[t - 1] if t else []):
                    attention(name)
            low_counts(NW - 1)
            for slot in SLOTS[NW - 1:]:
                for name in slot:
                    attention(name)
            dve.wait_ge(sem("s_bn1"), 1)
            own.after(n_deg[0])
            pend = []
            n = 0

            def finish_agg():
                f, ci, k, mark = pend.pop(0)
                c0, w = COLS[ci]
                own.after(mark)
                if k >= 4:
                    dve.wait_ge(sem("s_agl"), k - 3)
                dve.scalar_tensor_tensor(aggf[:, k % 4, 0:w], indb[:, c0:c0 + w], bn_t[:, f:f + 1],
                                         tmpr[:, k % 2, 0:w], ALU.mult, ALU.add).then_inc(sem("s_agf"), 1)

            for kind, f, ci in CONV:
                c0, w = COLS[ci]
                name = f"{kind}{f}{ci}"
                if kind == "A":
                    ps = read_group(dve, name)
                    if n >= 2:
                        dve.wait_ge(sem("s_agf"), n - 1)
                    mark = own.mark(dve.scalar_tensor_tensor(tmpr[:, n % 2, 0:w], ps[:, 0:w], bn_s[:, f:f + 1],
                                                             rdb[:, c0:c0 + w], ALU.mult, ALU.mult))
                    pend.append((f, ci, n, mark))
                    n += 1
                    finish_agg()
                    dve.sem_inc(free[PLACE[name][0]], 1)
                else:
                    ps = read_group(dve, name)
                    ins = dve.scalar_tensor_tensor(hT[:, f, c0:c0 + w], ps[:, 0:w], neg_bc[:, f:f + 1],
                                                   hT[:, f, c0:c0 + w], ALU.max, ALU.add)
                    free_group(ins, name)
                    dve.wait_ge(free[PLACE[name][0]], PLACE[name][1] + 1)
                    own.mark(feature_stats(f, ci, hT[:, f, c0:c0 + w]))
            own.after(own.n)
            for f in range(FB):
                own.mark(dve.bn_aggr(mv_f[:, f, :], st_f[:, f].rearrange("p c s -> p (c s)")))
            own.after(own.n)
            dve.sem_inc(sem("s_mv2"), 1)

            dve.wait_ge(sem("s_bn2"), 1)
            for j in range(N // PIECE):
                for f in (2, 3):
                    y = hT[:, f, j * PIECE:(j + 1) * PIECE]
                    dve.tensor_scalar(y, y, bn_s[:, f:f + 1], bn_t[:, f:f + 1], ALU.mult, ALU.add)\
                       .then_inc(sem("s_ynd"), 1)
            def low_rows(i):
                dve.wait_ge(sem("s_hb"), i + 1)
                dve.wait_ge(sem("s_hhb"), i + 1)
                dve.tensor_tensor(hl[:, i, :], hring1[:, i % 3, :], hh[:, i, :], ALU.subtract)\
                   .then_inc(sem("s_hlb"), 1)

            dve.wait_ge(sem("d_par"), 64)
            own.mark(dve.tensor_scalar(eps1[:], eps_col[:], 1.0, None, ALU.add))
            for i in range(T):
                if i % 5 == 0:
                    dve.wait_ge(sem(f"d_x1{i // 5}"), 16)
                ps = read_group(dve, f"x{i}")
                ins = dve.tensor_tensor(x1[:, i, :], ps[0:L, :], x1[:, i, :], ALU.add)
                free_group(ins, f"x{i}")
                dve.wait_ge(free[6], PLACE[f"x{i}"][1] + 1)
                own.step(dve.bn_stats(st_row[:, i % 2, :], x1[:, i, :]))
                dve.bn_aggr(mv_row[:, i, :], st_row[:, i % 2, :]).then_inc(sem("s_mvb"), 1)
                if i >= 2:
                    low_rows(i - 2)
                if i - 2 in W1_AT:
                    half = W1_AT.index(i - 2)
                    dve.wait_ge(sem("s_w1h"), half + 1)
                    dve.tensor_tensor(w1_lo[:, 2 * half:2 * half + 2, :], w1_s[:],
                                      w1_hi[:, 2 * half:2 * half + 2, :].bitcast(F32), ALU.subtract)\
                       .then_inc(sem("s_w1"), 1)
            low_rows(T - 2)
            low_rows(T - 1)

            own.after(own.n)
            for k, (f, ci) in enumerate(A1_FIRST + A1_REST):
                c0, w = COLS[ci]
                if k == 0:
                    dve.wait_ge(free[7], PLACE["g9"][1] + 1)
                ps = read_group(dve, f"B{f}{ci}")
                if k >= 4:
                    dve.wait_ge(sem("s_agl1"), k - 3)
                ins = dve.scalar_tensor_tensor(aggf[:, k % 4, 0:w], hT[:, f, c0:c0 + w], eps1[:, 0:1],
                                               ps[:, 0:w], ALU.mult, ALU.add).then_inc(sem("s_agf1"), 1)
                dve.wait_ge(sem("s_agf1"), k + 1)
                dve.sem_inc(free[PLACE[f"B{f}{ci}"][0]], 1)

            def z_stats(b, ci):
                c0, w = COLS[ci]
                bank, turn = PLACE[f"Z{b}{ci}"]
                dve.wait_ge(free[bank], turn + 1)
                own.mark(feature_stats(b, ci, zr[:, b % 2, c0:c0 + w]))

            def z_high(b):
                dve.wait_ge(sem("s_a"), b + 1)
                dve.tensor_copy(a_hi[:, b, :], zr[:, b % 2, :]).then_inc(sem("s_ah"), 1)

            def w2_low(f):
                dve.wait_ge(sem("s_w2h"), f + 1)
                dve.tensor_tensor(w2_lo[f][:], w2_s[f][:], w2_hi[f][:].bitcast(F32), ALU.subtract)\
                   .then_inc(sem("s_w2"), 1)

            for b in range(HB):
                z_stats(b, 0)
                if b:
                    z_high(b - 1)
                if b == 3:
                    w2_low(0)
                z_stats(b, 1)
                z_stats(b, 2)
                own.after(own.n)
                dve.bn_aggr(mv_f[:, b, :], st_f[:, b].rearrange("p c s -> p (c s)")).then_inc(sem("s_mvz"), 1)
            for ci, (c0, w) in enumerate(COLS):
                dve.wait_ge(sem("s_a"), HB + ci)
                z, hi = zr[:, (HB - 1) % 2, c0:c0 + w], a_hi[:, HB - 1, c0:c0 + w]
                own.step(dve.tensor_copy(hi, z))
                dve.tensor_tensor(a_lo[:, HB - 1, c0:c0 + w], z, hi.bitcast(F32), ALU.subtract)\
                   .then_inc(sem("s_al_last"), 1)
            w2_low(1)

            dve.wait_ge(sem("s_x1h"), T)

            def out_add(f, pieces):
                for j in pieces:
                    t0, t1 = OUT_TILES[j]
                    ps = read_group(dve, f"out{f}{j}")
                    o = x1[:, t0:t1, f * P:(f + 1) * P]
                    ins = dve.tensor_tensor(o, ps[0:L, 0:(t1 - t0) * P].rearrange("p (t d) -> p t d", d=P), o, ALU.add)
                    own.step(ins)
                    dve.sem_inc(free[PLACE[f"out{f}{j}"][0]], 1)
                    dve.sem_inc(sem("s_out"), 1)

            for f in range(FB):
                for ci in range(NC):
                    c0, w = COLS[ci]
                    bank, turn = PLACE[f"U{f}{ci}"]
                    dve.wait_ge(free[bank], turn + 1)
                    own.mark(feature_stats(f, ci, ur[:, f % 2, c0:c0 + w]))
                    if f and ci:
                        out_add(f - 1, ((0, 1), (2,))[ci - 1])
                own.after(own.n)
                dve.bn_aggr(mv_f[:, f, :], st_f[:, f].rearrange("p c s -> p (c s)")).then_inc(sem("s_mvu"), 1)
                if f == 0:
                    w2_low(2)
                    w2_low(3)
            out_add(FB - 1, range(3))

        @block.tensor
        def _(pe):
            def mm(o, l, r, start, stop):
                return pe.matmul(o, l, r, start=start, stop=stop, skip_group_check=True)

            pe.wait_ge(sem("s_const"), NCONST)
            pe.wait_ge(sem("s_prep"), 1)
            rest = NCH - P
            ps = open_group(pe, "codes")
            for a, k in enumerate((1, 2)):
                pe.transpose(ps[0:CH, a * NCH:a * NCH + P], code_r[:, k, 0, :], ident[:])
                ins = pe.transpose(ps[0:CH, a * NCH + P:(a + 1) * NCH], code_r[0:rest, k, 1, :],
                                   ident[0:rest, 0:rest])
            close_group(ins, "codes")
            ps = open_group(pe, "ranges")
            for a in range(2):
                mm(ps[0:NW, a * NCH:a * NCH + P], wm[:, a, 0:1].broadcast_to([P, NW]), ident[:], True, True)
                ins = mm(ps[0:NW, a * NCH + P:(a + 1) * NCH], wm[0:rest, a, 1:2].broadcast_to([rest, NW]),
                         ident[0:rest, 0:rest], True, True)
            close_group(ins, "ranges")
            def turn_rows(i, rows, slots, h_done, name):
                pe.wait_ge(sem(h_done), i + 1)
                ps = open_group(pe, name)
                for f in range(FB):
                    ins = pe.transpose(ps[:, f * L:(f + 1) * L], rows[:, i % slots, f * P:(f + 1) * P], ident[0:L, 0:L])
                close_group(ins, name)

            hT_ready = [False]

            def released(name):
                bank, turn = PLACE[name]
                pe.wait_ge(free[bank], turn + 1)

            def attention(name):
                if name == "SPAN":
                    pe.wait_ge(sem("s_span"), 1)
                    close_group(mm(open_group(pe, name)[0:1, 0:NW], rng_f[:, 3:4], ident[0:NW, 0:NW], True, True), name)
                    return
                if name[:2] == "hT":
                    turn_rows(int(name[2]), hring, HR, "s_h", name)
                    return
                if name[0] in "VQK" and name[:2] not in ("KV", "QT") and not hT_ready[0]:
                    for i in range(3):
                        released(f"hT{i}")
                    hT_ready[0] = True
                if name == "PT":
                    pe.wait_ge(sem("d_par"), 64)
                    ps = open_group(pe, name)
                    for a in range(2):
                        pe.transpose(ps[:, a * P:(a + 1) * P], proj_d[:, a, :], ident[:])
                    ins = pe.transpose(ps[:, M:M + NPAR], par_r[:], ident[0:NPAR, 0:NPAR])
                elif name[0] == "V":
                    nt = int(name[1])
                    pe.wait_ge(sem("d_wA"), 16)
                    ps = open_group(pe, name)
                    for k in range(FB):
                        ins = mm(ps[:], hT[:, k, nt * P:(nt + 1) * P], wA[:, k, :], k == 0, k == FB - 1)
                elif name in ("Q0", "Q1", "K0", "K1"):
                    w, d, n = (wA, "d_wA", 32) if name[0] == "Q" else (wB, "d_wB", 16)
                    pe.wait_ge(sem(d), n)
                    ps = open_group(pe, name)
                    for j in range(2):
                        f = 2 * int(name[1]) + j
                        for k in range(FB):
                            ins = mm(ps[:, j * MAXN:(j + 1) * MAXN], w[:, k, f * P:(f + 1) * P], hT[:, k, 0:MAXN],
                                     k == 0, k == FB - 1)
                elif name[0] == "D" and name != "DG":
                    c0, w = COLS[int(name[1])]
                    windows = -(-(c0 + w) // W)
                    pe.wait_ge(sem("s_at"), windows)
                    pe.wait_ge(sem("s_lo"), windows)
                    if name == "D0":
                        released("SPAN")
                        pe.load([most_r], most[0:1, 0:1])
                    ps = open_group(pe, name)
                    ins = accumulate([(ps[:, 0:w], [(ones16[0:L, :], AT[:, k, c0:c0 + w]) for k in range(T)],
                                       [(ones16[0:L, :], ATlo[:, k, c0:c0 + w]) for k in range(T)])])[0]
                elif name == "DG":
                    for q in ("Q0", "Q1", "K0", "K1"):
                        released(q)
                    ps = open_group(pe, name)
                    for a in range(2):
                        for f in range(FB):
                            for n in range(2):
                                c = 16 * a + 4 * f + n
                                ins = mm(ps[:, c:c + 3:2], sq[:, a, f, n * P:(n + 1) * P], half2[:], True, True)
                elif name[:2] in ("UQ", "UK"):
                    a, h = "QK".index(name[1]), int(name[2])
                    released(f"{name[1]}{h // 4}")
                    ps = open_group(pe, name)
                    p0 = DH * (h % 2)
                    for n in range(2):
                        ins = mm(ps[:, n * M:(n + 1) * M], tqk[p0:p0 + DH, a, h // 2, n * P:(n + 1) * P],
                                 projT[p0:p0 + DH, :], True, True)
                elif name[:2] == "KV":
                    g = int(name[2])
                    pe.wait_ge(sem("s_kf"), 2 * g + 2)
                    ps = open_group(pe, name)[:, 0:4 * (DH + 1)].rearrange("p (h m d) -> p h m d", h=2, m=2)
                    for j in range(2):
                        h = 2 * g + j
                        for m in range(2):
                            for n in range(2):
                                ins = mm(ps[:, j, m, :], kf[:, h % 4, n, m * P:(m + 1) * P], vaug[:, n, h, :],
                                         n == 0, n == 1)
                elif name[:2] == "QT":
                    h = int(name[2])
                    pe.wait_ge(sem("s_qf"), h + 1)
                    ps = open_group(pe, name)[:].rearrange("p (m n) -> p m n", m=2)
                    for m in range(2):
                        for n in range(2):
                            ins = pe.transpose(ps[:, m, n * P:(n + 1) * P], qf[:, h % 2, n, m * P:(m + 1) * P], ident[:])
                elif name[0] == "O":
                    g = int(name[1])
                    released(f"KV{g}")
                    released(f"QT{2 * g}")
                    released(f"QT{2 * g + 1}")
                    ps = open_group(pe, name)[:, 0:4 * (DH + 1)].rearrange("p (h n d) -> p h n d", h=2, n=2)
                    for j in range(2):
                        h = 2 * g + j
                        for n in range(2):
                            for m in range(2):
                                ins = mm(ps[:, j, n, :], qfT[:, h % 2, m, n * P:(n + 1) * P], kv[:, h, m, :],
                                         m == 0, m == 1)
                elif name[:2] == "AT":
                    nt = int(name[2])
                    released("O3")
                    ps = open_group(pe, name)
                    for f in range(FB):
                        ins = pe.transpose(ps[:, f * P:(f + 1) * P], attn[:, nt, f * P:(f + 1) * P], ident[:])
                elif name[:2] == "WO":
                    pe.wait_ge(sem("d_wB"), 32)
                    released("AT0")
                    released("AT1")
                    ps = open_group(pe, name)
                    for j in range(2):
                        f = 2 * int(name[2]) + j
                        for k in range(FB):
                            ins = mm(ps[:, j * MAXN:(j + 1) * MAXN], wB[:, k, f * P:(f + 1) * P], attnT[:, k, :],
                                     k == 0, k == FB - 1)
                close_group(ins, name)

            def accumulate(groups):
                for ps, pairs, _ in groups:
                    mm(ps, *pairs[0], True, False)
                with pe.If_lt(big_r, most_r):
                    for ps, _, extra in groups:
                        for l, r in extra:
                            mm(ps, l, r, False, False)
                pe.end_ifs()
                last = []
                for ps, pairs, _ in groups:
                    for n, (l, r) in enumerate(pairs[1:]):
                        ins = mm(ps, l, r, False, n == len(pairs) - 2)
                    last.append(ins)
                return last

            seen = pe.alloc_register("seen")
            lo_r, hi_r = pe.alloc_register("first_chunk_pe"), pe.alloc_register("last_chunk_pe")
            most_r, big_r = pe.alloc_register("most_chunks"), pe.alloc_register("exact_chunks_pe")
            pe.reg_mov(big_r, BIG)
            pe.reg_mov(seen, 0)
            pe.wait_ge(sem("s_ranges"), 1)
            pe.sem_inc(sem("s_slot"), G)
            rest_r = pe.alloc_register("further_chunks_pe")

            def count_body(ps, i, opens):
                for j in range(G):
                    if j % Q == 0:
                        pe.reg_add(seen, seen, 1)
                        pe.wait_ge(sem("s_hot"), pe.snap(seen, min_val=1, max_val=1 << 20))
                    ins = mm(ps[:, 0:CODES], S[:, :, bass.ds(i + j, 1)].rearrange("e l c -> e (l c)"),
                             ring[:, j, :], opens and j == 0, False)
                    if j % Q == Q - 1:
                        ins.then_inc(sem("s_slot"), Q)

            for t in range(NW):
                pe.load([lo_r, hi_r], ranges[t:t + 1, :])
                lo, hi = pe.snap(lo_r, min_val=0, max_val=NCH - 1), pe.snap(hi_r, min_val=1, max_val=NCH)
                if t >= 2:
                    pe.wait_ge(sem("s_at"), t - 1)
                    pe.wait_ge(sem("s_lo"), t - 1)
                ps = banks[t % 2]
                count_body(ps, lo, True)
                pe.reg_add(rest_r, lo_r, G)
                with pe.If_lt(rest_r, hi_r):
                    with pe.Fori(pe.snap(rest_r, min_val=G, max_val=NCH), hi, G) as i:
                        count_body(ps, i, False)
                pe.end_ifs()
                mm(ps[:, 0:1], ones16[0:CH, :], zeros16[0:CH, 0:1], False, True).then_inc(sem("s_win"), 1)
                for name in SLOTS[t]:
                    attention(name)
            for slot in SLOTS[NW:]:
                for name in slot:
                    attention(name)

            pe.wait_ge(sem("s_at"), NW)
            pe.wait_ge(sem("s_lo"), NW)
            pe.wait_ge(sem("s_hl"), T)

            def split3(ps, w, wts, acts, ks):
                (w_hi, w_lo), (x_hi, x_lo) = wts, acts
                n = 0
                for k in ks:
                    for a, b in ((w_hi, x_hi), (w_hi, x_lo), (w_lo, x_hi)):
                        ins = mm(ps[:, 0:w], a(k), b(k), n == 0, n == 3 * len(ks) - 1)
                        n += 1
                return ins

            def aggregate(kind, blocks, ci):
                c0, w = COLS[ci]
                groups = []
                for f in blocks:
                    ps, fs = open_group(pe, f"{kind}{f}{ci}"), slice(f * P, (f + 1) * P)
                    groups.append((ps[:, 0:w],
                                   [(h[:, k, fs], AT[:, k, c0:c0 + w]) for k in range(T) for h in (hh, hl)],
                                   [(h[:, k, fs], ATlo[:, k, c0:c0 + w]) for k in range(T) for h in (hh, hl)]))
                for f, ins in zip(blocks, accumulate(groups)):
                    close_group(ins, f"{kind}{f}{ci}")

            for kind, f, ci in CONV:
                c0, w = COLS[ci]
                name = f"{kind}{f}{ci}"
                if kind == "A":
                    if f == 0:
                        aggregate("A", range(FB), ci)
                else:
                    pe.wait_ge(sem("s_wc"), 1)
                    pe.wait_ge(sem("s_agl"), FB * (ci + 1))
                    ps = open_group(pe, name)
                    fs = slice(f * P, (f + 1) * P)
                    ins = split3(ps, w, (lambda k: wc_hi[:, k, fs], lambda k: wc_lo[:, k, fs]),
                                 (lambda k: agg_hi[:, k, c0:c0 + w], lambda k: agg_lo[:, k, c0:c0 + w]), range(FB))
                    close_group(ins, name)

            def agg1_rows(k):
                pe.wait_ge(sem("s_hlb"), k + 1)
                for f, ci in A1_FIRST:
                    c0, w = COLS[ci]
                    name = f"B{f}{ci}"
                    ps = open_group(pe, name) if k == 0 else banks[PLACE[name][0]]
                    fs = slice(f * P, (f + 1) * P)
                    mm(ps[:, 0:w], hh[:, k, fs], AT[:, k, c0:c0 + w], k == 0, False)
                    ins = mm(ps[:, 0:w], hl[:, k, fs], AT[:, k, c0:c0 + w], False, k == T - 1)
                    if k == T - 1:
                        close_group(ins, name)

            def agg1_extra():
                pe.wait_ge(sem("s_hlb"), T)
                with pe.If_lt(big_r, most_r):
                    for f, ci in A1_FIRST:
                        c0, w = COLS[ci]
                        fs = slice(f * P, (f + 1) * P)
                        for k in range(T):
                            for h in (hh, hl):
                                mm(banks[PLACE[f"B{f}{ci}"][0]][:, 0:w], h[:, k, fs], ATlo[:, k, c0:c0 + w], False, False)
                pe.end_ifs()

            for i in range(T):
                pe.wait_ge(sem("s_yna"), 2 * (i // 2 + 1))
                pe.wait_ge(sem("s_ynd"), 2 * (i // 2 + 1))
                ps = open_group(pe, f"x{i}")
                for f in range(FB):
                    ins = pe.transpose(ps[0:L, f * P:(f + 1) * P], hT[:, f, i * L:(i + 1) * L], ident[:])
                close_group(ins, f"x{i}")
                if i >= 2:
                    turn_rows(i - 2, hring1, 3, "s_hb", f"g{i - 2}")
                if i >= 3:
                    agg1_rows(i - 3)
            for i in (T - 2, T - 1):
                turn_rows(i, hring1, 3, "s_hb", f"g{i}")
                agg1_rows(i - 1)
            agg1_extra()
            agg1_rows(T - 1)
            for ci in range(NC):
                aggregate("B", (2, 3), ci)

            pe.wait_ge(sem("s_w1"), 2)
            for b in range(HB):
                for ci in range(NC):
                    c0, w = COLS[ci]
                    if b == 0:
                        pe.wait_ge(sem("s_agl1"), len(A1_FIRST) + 2 * (ci + 1))
                    ps = open_group(pe, f"Z{b}{ci}")
                    bs = slice(b * P, (b + 1) * P)
                    ins = split3(ps, w, (lambda k: w1_hi[:, k, bs], lambda k: w1_lo[:, k, bs]),
                                 (lambda k: agg_hi[:, k, c0:c0 + w], lambda k: agg_lo[:, k, c0:c0 + w]), range(FB))
                    close_group(ins, f"Z{b}{ci}")

            def out_rows(f, pieces):
                for j in pieces:
                    t0, t1 = OUT_TILES[j]
                    pe.wait_ge(sem("s_o"), 3 * f + j + 1)
                    ps = open_group(pe, f"out{f}{j}")
                    for i in range(t0, t1):
                        ins = pe.transpose(ps[0:L, (i - t0) * P:(i - t0 + 1) * P],
                                           orr[:, f % 2, i * L:(i + 1) * L], ident[:])
                    close_group(ins, f"out{f}{j}")

            for f in range(FB):
                pe.wait_ge(sem("s_w2"), f + 1)
                if f == 0:
                    for k in range(HB):
                        for ci in range(NC):
                            if k < HB - 1:
                                pe.wait_ge(sem("s_al"), k + 1)
                            else:
                                pe.wait_ge(sem("s_al_last"), ci + 1)
                            c0, w = COLS[ci]
                            ps = open_group(pe, f"U{f}{ci}") if k == 0 else banks[PLACE[f"U{f}{ci}"][0]]
                            for n, (a, b) in enumerate(((w2_hi[0], a_hi), (w2_hi[0], a_lo), (w2_lo[0], a_hi))):
                                ins = mm(ps[:, 0:w], a[:, k, :], b[:, k, c0:c0 + w], k == n == 0, k == HB - 1 and n == 2)
                            if k == HB - 1:
                                close_group(ins, f"U{f}{ci}")
                    continue
                for ci in range(NC):
                    c0, w = COLS[ci]
                    ps = open_group(pe, f"U{f}{ci}")
                    ins = split3(ps, w, (lambda k: w2_hi[f][:, k, :], lambda k: w2_lo[f][:, k, :]),
                                 (lambda k: a_hi[:, k, c0:c0 + w], lambda k: a_lo[:, k, c0:c0 + w]), range(HB))
                    close_group(ins, f"U{f}{ci}")
                    if ci:
                        out_rows(f - 1, ((0, 1), (2,))[ci - 1])
            out_rows(FB - 1, range(3))


def kernel(**inputs):
    import numpy as _np
    import concourse.bacc as _bacc
    from concourse import mybir as _mybir
    from concourse.bass_utils import run_bass_kernel_spmd as _run

    def get(name):
        return _np.ascontiguousarray(inputs[name])

    p0, p1 = "L0_gnn_", "L1_gnn_"
    names = [p0 + "norm1_g", p0 + "norm1_b", p0 + "norm2_g", p0 + "norm2_b", p0 + "b_conv",
             p1 + "b1", p1 + "g1", p1 + "be1", p1 + "b2", p1 + "g2", p1 + "be2"]
    arrays = {
        "x": get("x"), "src": get("src"), "dst": get("dst"),
        "params": _np.concatenate([get(n) for n in names]).reshape(NPAR, P),
        "eps": get(p1 + "eps").reshape(1, 1),
        "w_conv": get(p0 + "W_conv"), "wq": get(p0 + "Wq"), "wk": get(p0 + "Wk"), "wv": get(p0 + "Wv"),
        "wo": get(p0 + "Wo"), "proj": get(p0 + "proj"), "w1": get(p1 + "W1"), "w2": get(p1 + "W2"),
    }
    nc = _bacc.Bacc("TRN2", target_bir_lowering=False, num_devices=1)
    args = {k: nc.dram_tensor(k, a.shape, _mybir.dt.from_np(a.dtype), kind="ExternalInput").ap()
            for k, a in arrays.items()}
    o = nc.dram_tensor("out", (N, D), _mybir.dt.float32, kind="ExternalOutput").ap()
    gnn_kernel(nc, out=o, **args)
    r = _run(nc, [arrays], core_ids=[0])
    return r.results[0]["out"]
```
